# Optimizing a Trainium2 kernel written in Bass

```python
import numpy as np
import jax
import jax.numpy as jnp

def _softmax(x, axis=-1):
    return jax.nn.softmax(x, axis=axis)

def _gelu(x):
    return jax.nn.gelu(x, approximate=True)

def _silu(x):
    return jax.nn.silu(x)

def _sigmoid(x):
    return jax.nn.sigmoid(x)

def _layernorm(x, axis=-1, eps=1e-05):
    m = jnp.mean(x, axis=axis, keepdims=True)
    v = jnp.var(x, axis=axis, keepdims=True)
    return (x - m) / jnp.sqrt(v + eps)

def _scatter_add(tgt, idx, src, axis=0):
    return tgt.at[idx].add(src)

def _segment_sum(src, seg, n):
    return jax.ops.segment_sum(src, seg, n)
kernel_name = 'mk_prb_d1_jaxref_r8_9ae71d'

def setup_inputs(seed: int=0):
    np.random.seed(seed)
    _w = jnp.asarray

    def _L0_attn_setup():
        import jax, jax.numpy as jnp
        import numpy as np
        IN_DIM = 128
        OUT_DIM = 128
        key = jax.random.key(seed)
        ks = jax.random.split(key, 7)
        B, S = (4, 256)
        x = jax.random.normal(ks[0], (B, S, IN_DIM), dtype=jnp.float32)
        s = 1.0 / np.sqrt(IN_DIM)
        Wk = jax.random.uniform(ks[1], (OUT_DIM, IN_DIM), minval=-s, maxval=s, dtype=jnp.float32)
        Wq = jax.random.uniform(ks[2], (OUT_DIM, IN_DIM), minval=-s, maxval=s, dtype=jnp.float32)
        Wv = jax.random.uniform(ks[3], (OUT_DIM, IN_DIM), minval=-s, maxval=s, dtype=jnp.float32)
        bk = jax.random.uniform(ks[4], (OUT_DIM,), minval=-s, maxval=s, dtype=jnp.float32)
        bq = jax.random.uniform(ks[5], (OUT_DIM,), minval=-s, maxval=s, dtype=jnp.float32)
        bv = jax.random.uniform(ks[6], (OUT_DIM,), minval=-s, maxval=s, dtype=jnp.float32)
        return {'x': x, 'Wk': Wk, 'bk': bk, 'Wq': Wq, 'bq': bq, 'Wv': Wv, 'bv': bv}
    _L0_attn_in = _L0_attn_setup()

    def _L0_ffn_setup():
        import jax, jax.numpy as jnp
        import numpy as np
        D_MODEL = 128
        D_HIDDEN = 512
        NUM_BANKS = 16
        NUM_SELECTED = 2
        key = jax.random.key(seed)
        ks = jax.random.split(key, 7)
        s = 0.02
        return {'tensor': jax.random.normal(ks[0], (4, 128, D_MODEL), dtype=jnp.float32), 'Wr': jax.random.normal(ks[1], (D_MODEL, NUM_BANKS), dtype=jnp.float32) * s, 'br': jnp.zeros((NUM_BANKS,), dtype=jnp.float32), 'W1': jax.random.normal(ks[2], (NUM_BANKS, D_MODEL, D_HIDDEN), dtype=jnp.float32) * s, 'b1': jnp.zeros((NUM_BANKS, D_HIDDEN), dtype=jnp.float32), 'W2': jax.random.normal(ks[3], (NUM_BANKS, D_HIDDEN, D_MODEL), dtype=jnp.float32) * s, 'b2': jnp.zeros((NUM_BANKS, D_MODEL), dtype=jnp.float32)}
    _L0_ffn_in = _L0_ffn_setup()
    _d = {'L0_attn_x': _L0_attn_in['x'], 'L0_attn_Wk': _L0_attn_in['Wk'], 'L0_attn_bk': _L0_attn_in['bk'], 'L0_attn_Wq': _L0_attn_in['Wq'], 'L0_attn_bq': _L0_attn_in['bq'], 'L0_attn_Wv': _L0_attn_in['Wv'], 'L0_attn_bv': _L0_attn_in['bv'], 'L0_ffn_Wr': _L0_ffn_in['Wr'], 'L0_ffn_br': _L0_ffn_in['br'], 'L0_ffn_W1': _L0_ffn_in['W1'], 'L0_ffn_b1': _L0_ffn_in['b1'], 'L0_ffn_W2': _L0_ffn_in['W2'], 'L0_ffn_b2': _L0_ffn_in['b2']}
    _x0 = _d['L0_attn_x']
    _d['L0_attn_x'] = jax.random.normal(jax.random.fold_in(jax.random.key(seed), 1), (2, 1024, 128), dtype=_x0.dtype)
    del _x0
    return _d

def reference(L0_attn_x, L0_attn_Wk, L0_attn_bk, L0_attn_Wq, L0_attn_bq, L0_attn_Wv, L0_attn_bv, L0_ffn_Wr, L0_ffn_br, L0_ffn_W1, L0_ffn_b1, L0_ffn_W2, L0_ffn_b2):

    def _L0_attn_ref(x, Wk, bk, Wq, bq, Wv, bv):
        import jax, jax.numpy as jnp
        import numpy as np
        IN_DIM = 128
        OUT_DIM = 128
        k = jnp.einsum('bsi,oi->bso', x, Wk) + bk
        q = jnp.einsum('bsi,oi->bso', x, Wq) + bq
        v = jnp.einsum('bsi,oi->bso', x, Wv) + bv
        d = k.shape[-1]
        scores = jnp.einsum('bqd,bkd->bqk', q, k) * d ** (-0.5)
        S = x.shape[1]
        causal = jnp.tril(jnp.ones((S, S), dtype=bool))
        scores = jnp.where(causal, scores, -jnp.inf)
        attn = jax.nn.softmax(scores, axis=-1)
        return jnp.einsum('bqk,bkd->bqd', attn, v)

    def _L0_ffn_ref(tensor, Wr, br, W1, b1, W2, b2):
        import jax, jax.numpy as jnp
        import numpy as np
        D_MODEL = 128
        D_HIDDEN = 512
        NUM_BANKS = 16
        NUM_SELECTED = 2
        logits = jnp.einsum('bsd,de->bse', tensor, Wr) + br
        probs = jax.nn.softmax(logits, axis=-1)
        topv, topi = jax.lax.top_k(probs, NUM_SELECTED)
        gate = jnp.sum(jax.nn.one_hot(topi, NUM_BANKS, dtype=tensor.dtype) * topv[..., None], axis=-2)
        h = jax.nn.relu(jnp.einsum('bsd,edh->bseh', tensor, W1) + b1)
        y = jnp.einsum('bseh,ehm->bsem', h, W2) + b2
        out = jnp.einsum('bse,bsem->bsm', gate, y)
        return out
    x = L0_attn_x
    xn = _layernorm(x, axis=-1)
    x = x + _L0_attn_ref(xn, L0_attn_Wk, L0_attn_bk, L0_attn_Wq, L0_attn_bq, L0_attn_Wv, L0_attn_bv) + _L0_ffn_ref(xn, L0_ffn_Wr, L0_ffn_br, L0_ffn_W1, L0_ffn_b1, L0_ffn_W2, L0_ffn_b2)
    return x

_drawn_inputs = setup_inputs


def setup_inputs(seed=0):
    import zlib

    import numpy as np

    out = dict(_drawn_inputs(seed))
    spreads = {'L0_ffn_br': (0.0, 0.617), 'L0_ffn_b1': (0.0, 0.8), 'L0_ffn_b2': (0.0, 0.621)}
    factors = {'L0_attn_bk': 64.0,
     'L0_attn_bq': 30.672,
     'L0_ffn_Wr': 3.811,
     'L0_ffn_W1': 7.095,
     'L0_ffn_W2': 5.466,
     'L0_attn_Wq': 3.09}
    for name, (base, spread) in spreads.items():
        noise = np.random.default_rng([zlib.crc32(name.encode()), seed]).standard_normal(out[name].shape)
        drawn = base * np.exp(spread * noise) if base else spread * noise
        out[name] = jnp.asarray(drawn.astype(out[name].dtype))
    for name, factor in factors.items():
        out[name] = (out[name] * factor).astype(out[name].dtype)
    return out
```

```python
from contextlib import ExitStack

import concourse.bass as bass
from concourse import mybir

ALU = mybir.AluOpType
ACT = mybir.ActivationFunctionType
AX = mybir.AxisListType
F32 = mybir.dt.float32
F16 = mybir.dt.float16
I32 = mybir.dt.int32

P = 128
HUGE = 3.0e38


def attention_and_top2_experts(nc, x, Wk, bk, Wq, bq, Wv, bv, Wr, br, W1, b1, W2, b2, out):
    B, S, D = x.shape
    E = Wr.shape[1]
    HID = W1.shape[2]
    K = 2
    NT = B * S // P
    TB = S // P
    NCH = HID // P
    TILES = K * NT + E - 1
    EPS = 1e-5
    SCALE = float(D) ** -0.5
    G = 4
    NG = NT // G
    assert D == P and HID == NCH * P

    ROW = 2 * D + 4
    W2_HI, W2_LO, SEL, B2F, CF = 0, HID, 2 * HID, (2 * HID + P) // 2, (2 * HID + P) // 2 + D
    KIT = 2 * (CF + 1)
    RAW = 6
    WG = 4
    POOL_HI = 8
    NST, NHB, NYB = 3, 3, 4
    XG = 12
    NXG = -(-TILES // XG)
    NYL = 4
    TYL = NT // NYL

    slots_dram = nc.dram_tensor("slots_dram", (P * TILES, ROW), F16).ap()
    pairs_dram = nc.dram_tensor("pairs_dram", (NT * P * K, D), F32).ap()

    with ExitStack() as ctx:
        def sb(name, shape, dt):
            return ctx.enter_context(nc.sbuf_tensor(name, shape, dt))

        def sem(name):
            return ctx.enter_context(nc.semaphore(name))

        xin = sb("xin", [P, NT, D], F32)
        xn = sb("xn", [P, NT, D], F32)
        xT = sb("xT", [P, NT * P], F32)
        qT = sb("qT", [P, NT * P], F32)
        kT = sb("kT", [P, NT * P], F32)
        v = sb("v", [P, NT, D], F32)
        w1 = sb("w1", [P, E, 2, HID], F16)
        kits = sb("kits", [P, E, KIT], F16)
        raw = sb("raw", [P, RAW, 2, HID], F32)
        probsT = sb("probsT", [P, 2, G * P], F32)
        wr = sb("wr", [P, E], F32)
        brb = sb("brb", [P, E], F32)
        bqk = sb("bqk", [P, 2], F32)
        bvb = sb("bvb", [P, D], F32)
        b1rows = sb("b1rows", [P, HID], F32)
        b1parts = sb("b1parts", [P, HID], F16)
        stats = sb("stats", [P, NT, 6], F32)
        mv = sb("mv", [P, NT, 2], F32)
        std = sb("std", [P, NT], F32)
        rstd = sb("rstd", [P, NT], F32)
        epsc = sb("epsc", [P, 1], F32)
        ident = sb("ident", [P, P], F32)
        ident16 = sb("ident16", [P, P], F16)
        causal = sb("causal", [P, P], F32)
        before = sb("before", [P, P], F16)
        ones16 = sb("ones16", [P, P], F16)
        ones = sb("ones", [P, P], F32)
        tileno = sb("tileno", [P, TILES + 1], F32)
        scratch_i = sb("scratch_i", [P, TILES + 1], I32)
        blank = sb("blank", [P, ROW], F16)
        chosen = sb("chosen", [P, E, NT], F16)
        best = sb("best", [P, K, NT], F32)
        pick = sb("pick", [P, NT], F32)
        exsum = sb("exsum", [P, NT], F32)
        gap = sb("gap", [P, NT], F32)
        gate = sb("gate", [P, K, NT], F32)
        posk = sb("posk", [P, K, NT], F32)
        posi = sb("posi", [P, K, NT], I32)
        posr = sb("posr", [P, K, NT], I32)
        slotrow = sb("slotrow", [P, K, NT], I32)
        cnt = sb("cnt", [P, E], I32)
        ntile = sb("ntile", [P, E], I32)
        ntilef = sb("ntilef", [P, E], F32)
        cum = sb("cum", [P, E], F32)
        start = sb("start", [P, E], F32)
        expertf = sb("expertf", [1, TILES + 1], F32)
        expert = sb("expert", [1, TILES + 1], I32)
        sumsq = sb("sumsq", [P, 3, E], F32)
        nrm = sb("nrm", [P, 3, E], F32)
        nrmi = sb("nrmi", [P, 3, E], I32)
        nrmi2 = sb("nrmi2", [P, 3, E], I32)
        pw = sb("pw", [P, 3, E], I32)
        bound = sb("bound", [P, E], F32)
        pb = sb("pb", [P, 2, E], I32)
        inv = sb("inv", [P, 2, E], F32)
        wscale = sb("wscale", [P, 2, E], F32)
        b1s = sb("b1s", [P, 1], F32)
        b1tmp = sb("b1tmp", [P, E], F32)
        m0 = sb("m0", [P, NT], F32)
        m1 = sb("m1", [P, NT], F32)
        negm = sb("negm", [P, NT], F32)
        rsum = sb("rsum", [P, NT], F32)
        rinv = sb("rinv", [P, NT], F32)

        slot_space = sb("slot_space", [P, TILES * ROW], F16)
        slots = slot_space[:, :].rearrange("p (t c) -> p t c", t=TILES)
        rows = slot_space[:, 0:K * NT * ROW].rearrange("p (k t c) -> p k t c", k=K, t=NT)

        stage_w, hid_w, xslot_w, ybuf_w = NST * KIT, NHB * 2 * HID, 3 * 2 * D, NYB * 2 * D
        space = sb("space", [P, stage_w + hid_w + xslot_w + ybuf_w], F16)
        stage = space[:, 0:stage_w].rearrange("p (s c) -> p s c", s=NST)
        hid = space[:, stage_w:stage_w + hid_w].rearrange("p (s a h) -> p s a h", s=NHB, a=2)
        at = stage_w + hid_w
        xslot = space[:, at:at + xslot_w].rearrange("p (s c) -> p s c", s=3)
        at += xslot_w
        ybuf = space[:, at:at + ybuf_w].bitcast(F32).rearrange("p (s d) -> p s d", s=NYB)

        taken = [0]

        def early(n, parts=P):
            a = 2 * taken[0]
            taken[0] += n
            assert 2 * taken[0] <= stage_w + hid_w + xslot_w + ybuf_w
            return space[0:parts, a:a + 2 * n].bitcast(F32)

        def per_expert(n=1):
            return early(n * E * NT).rearrange("p (e t) -> p e t", t=NT)

        wqkv = early(3 * D).rearrange("p (n d) -> p n d", n=3)
        wqkvT = early(3 * D).rearrange("p (n d) -> p n d", n=3)
        b1cols = early(E * NCH).rearrange("p (e c) -> p e c", e=E)
        b1sq = early(E * NCH).rearrange("p (e c) -> p e c", e=E)
        rev, keep = per_expert(), per_expert()
        lg, lg2, hit, ex, incl, pos = (per_expert() for _ in range(6))
        oh = early(K * E * NT).rearrange("p (k e t) -> p k e t", k=K, e=E)
        past = early((TILES + 1) * E, 1).rearrange("p (t e) -> p t e", e=E)

        probs = xn[:, :, :].rearrange("p t d -> p (t d)").rearrange("p (a n) -> p a n", a=2)
        pairs = raw[:, 0:4, :, :].rearrange("p r w h -> p (r w h)").rearrange(
            "p (t k d) -> p t k d", k=K, d=D)
        slots_i = slot_space[:, :].bitcast(I32).rearrange(
            "p (t c) -> p t c", t=TILES)
        rows_i = slot_space[:, 0:K * NT * ROW].bitcast(I32).rearrange(
            "p (k t c) -> p k t c", k=K, t=NT)
        kits_f = kits[:, :, :].rearrange("p e c -> p (e c)").bitcast(F32).rearrange(
            "p (e c) -> p e c", e=E)
        stage_f = space[:, 0:stage_w].bitcast(F32).rearrange(
            "p (s c) -> p s c", s=NST)

        kits_i = kits[:, :, :].rearrange("p e c -> p (e c)").bitcast(I32).rearrange(
            "p (e c) -> p e c", e=E)
        stage_i = space[:, 0:stage_w].bitcast(I32).rearrange("p (s c) -> p s c", s=NST)

        pS = [ctx.enter_context(nc.psum_tensor(f"pS{n}", [P, 1024], F32)) for n in range(2)]
        pT = [ctx.enter_context(nc.psum_tensor(f"pT{n}", [P, 512], F32)) for n in range(2)]
        pO = [ctx.enter_context(nc.psum_tensor(f"pO{n}", [P, 512], F32)) for n in range(2)]

        def pA(n):
            return pS[n % 4 // 2][:, 512 * (n % 2):512 * (n % 2) + 512]

        x_in = [sem(f"x_in{g}") for g in range(NG)]
        small_in = sem("small_in")
        bias_in = sem("bias_in")
        b2_in = sem("b2_in")
        w_in = [sem(f"w_in{n}") for n in range(E // 2)]
        blank_sent = sem("blank_sent")
        rows_sent = sem("rows_sent")
        slots_in = [sem(f"slots_in{n}") for n in range(NXG)]
        staged = [sem(f"staged{n}") for n in range(NST)]
        y_sent = [sem(f"y_sent{n}") for n in range(NYB)]
        pairs_in = [sem(f"pairs_in{n}") for n in range(NYL)]
        out_sent = sem("out_sent")
        consts = sem("consts")
        pool_step = sem("pool_step")
        dve_step = sem("dve_step")
        wT_done = sem("wT_done")
        wT_copied = sem("wT_copied")
        var_done = sem("var_done")
        std_done = sem("std_done")
        xn_done = sem("xn_done")
        xT_done = sem("xT_done")
        xT_copied = sem("xT_copied")
        hi_rows = sem("hi_rows")
        rows_done = sem("rows_done")
        logits_done = sem("logits_done")
        chosen_done = sem("chosen_done")
        ranks_done = sem("ranks_done")
        slotrow_done = sem("slotrow_done")
        expert_done = sem("expert_done")
        gap_done = sem("gap_done")
        ex_done = sem("ex_done")
        proj_done = sem("proj_done")
        proj_copied = sem("proj_copied")
        xbv_done = sem("xbv_done")
        sq_done = sem("sq_done")
        sums_done = sem("sums_done")
        sums_read = sem("sums_read")
        scale_done = sem("scale_done")
        whi_pool = sem("whi_pool")
        whi_act = sem("whi_act")
        wlo_done = sem("wlo_done")
        b1_done = sem("b1_done")
        s_done = sem("s_done")
        max_done = sem("max_done")
        exp_done = sem("exp_done")
        pt_done = sem("pt_done")
        pt_act = sem("pt_act")
        pt_dve = sem("pt_dve")
        o_done = sem("o_done")
        o_read = sem("o_read")
        xs_done = sem("xs_done")
        xs_copied = sem("xs_copied")
        l1_done = sem("l1_done")
        hi_done = sem("hi_done")
        lo_done = sem("lo_done")
        l2_done = sem("l2_done")
        y_done = sem("y_done")
        res_done = sem("res_done")

        x_v = x.rearrange("b (t p) d -> p (b t) d", p=P)
        out_v = out.rearrange("b (t p) d -> p (b t) d", p=P)
        slots_v = slots_dram.rearrange("(p t) c -> p t c", p=P)
        pairs_v = pairs_dram.rearrange("(t p k) d -> p t k d", p=P, k=K)
        w1_v = W1.rearrange("e d h -> d e h")
        w2_v = W2.rearrange("e (p c) m -> p e (c m)", p=P)

        N_CONST = 4

        block = ctx.enter_context(nc.Block())

        def groups_until(t):
            return sum(-(-(u % TB + 1) // G) for u in range(t))

        @block.sync
        def _(sp):
            for g in range(NG):
                sp.dma_start(xin[:, G * g:G * g + G, :], x_v[:, G * g:G * g + G, :]).then_inc(x_in[g], 16)
            for n, w in enumerate((Wq, Wk, Wv)):
                sp.dma_start(wqkv[:, n, :], w).then_inc(small_in, 16)
            sp.dma_start(wr[:, :], Wr).then_inc(small_in, 16)
            sp.wait_ge(consts, N_CONST)
            sp.dma_start(slots_v, blank[:, None, :].broadcast_to([P, TILES, ROW])).then_inc(blank_sent, 16)
            for n in range(E // 2):
                if 2 * n >= RAW:
                    sp.wait_ge(wlo_done, 2 * (2 * n - RAW + 2))
                r = 2 * n % RAW
                sp.dma_start(raw[:, r:r + 2, 0, :], w1_v[:, 2 * n:2 * n + 2, :]).then_inc(w_in[n], 16)
                sp.dma_start(raw[:, r:r + 2, 1, :], w2_v[:, 2 * n:2 * n + 2, :]).then_inc(w_in[n], 16)
            sp.wait_ge(rows_sent, 16 * K * NT)
            for n in range(NXG):
                a, z = XG * n, min(XG * n + XG, TILES)
                sp.dma_start(slots[:, a:z, :], slots_v[:, a:z, :]).then_inc(slots_in[n], 16)
            sp.wait_ge(expert_done, 1)
            sp.wait_ge(wlo_done, 2 * E)
            sp.wait_ge(b2_in, 16)
            for j in range(TILES):
                e = nc.s_assert_within(
                    sp.value_load(expert[0:1, j:j + 1]), 0, E - 1,
                    skip_runtime_bounds_check_because="a count of experts, held to E - 1 by a min")
                if j >= NST:
                    sp.wait_ge(y_done, j - NST + 1)
                sp.dma_start(stage_i[:, j % NST, :],
                             kits_i[:, bass.ds(e, 1), :].rearrange("p a c -> p (a c)")).then_inc(staged[j % NST], 16)
            for n in range(NYB):
                sp.wait_ge(y_sent[n], 16 * len(range(n, TILES, NYB)))
            for n in range(NYL):
                sp.dma_start(pairs[:, TYL * n:TYL * n + TYL, :, :],
                             pairs_v[:, TYL * n:TYL * n + TYL, :, :]).then_inc(pairs_in[n], 16)
            for n in range(NYL):
                sp.wait_ge(res_done, n + 1)
                sp.dma_start(out_v[:, TYL * n:TYL * n + TYL, :], xin[:, TYL * n:TYL * n + TYL, :]).then_inc(out_sent, 16)
            sp.wait_ge(out_sent, 16 * NYL)

        @block.gpsimd
        def _(pool):
            made = [0]

            def step(ins):
                made[0] += 1
                ins.then_inc(pool_step, 1)
                pool.wait_ge(pool_step, made[0])

            pool.memset(ident[:, :], 0.0)
            pool.memset(causal[:, :], 0.0)
            pool.memset(before[:, :], 1.0)
            pool.memset(ones16[:, :], 1.0)
            pool.memset(blank[:, :], 0.0)
            step(pool.memset(ones[:, :], 1.0))
            pool.affine_select(out=ident[:, :], in_=ident[:, :], compare_op=ALU.not_equal, fill=1.0,
                               base=0, pattern=[[-1, P]], channel_multiplier=1)
            pool.iota(blank[:, :].bitcast(I32)[:, D:D + 1], pattern=[[0, 1]], base=1 << 20, channel_multiplier=0)
            step(pool.affine_select(out=before[:, :], in_=before[:, :], compare_op=ALU.is_gt, fill=0.0,
                                    base=0, pattern=[[1, P]], channel_multiplier=-1))
            pool.tensor_copy(ident16[:, :], ident[:, :]).then_inc(consts, 1)
            pool.affine_select(out=causal[:, :], in_=causal[:, :], compare_op=ALU.is_ge, fill=-HUGE,
                               base=0, pattern=[[-1, P]], channel_multiplier=1).then_inc(consts, 1)
            for k in range(K):
                pool.iota(rows_i[:, k, :, D:D + 2], pattern=[[K * P, NT], [0, 2]], base=k, channel_multiplier=K)
            step(pool.iota(scratch_i[:, :], pattern=[[1, TILES + 1]], base=0, channel_multiplier=0))
            pool.tensor_copy(tileno[:, :], scratch_i[:, :]).then_inc(consts, 1)
            for e in range(E):
                pool.memset(rev[:, e, :], float(E - e))
            pool.memset(keep[:, :, 1:NT], 1.0)
            pool.memset(b1parts[:, :], 0.0)
            pool.memset(kits[:, :, SEL:SEL + P], 0.0)
            step(pool.memset(keep[:, :, 0:1], 0.0))
            sel = kits[:, :, SEL:SEL + P]
            for half in range(2):
                step(pool.affine_select(out=sel, in_=sel, compare_op=ALU.not_equal, fill=1.0,
                                        base=-32 * half, pattern=[[-1, E], [0, P]], channel_multiplier=1))
            pool.memset(epsc[:, :], EPS).then_inc(consts, 1)
            pool.wait_ge(bias_in, 16 * 7)
            for g in range(NG):
                pool.wait_ge(xn_done, g + 1)
                for t in range(G * g, G * g + G):
                    pool.tensor_tensor(xin[:, t, :], xin[:, t, :], bvb[:, :], ALU.add).then_inc(xbv_done, 1)
            for e in range(POOL_HI):
                pool.wait_ge(scale_done, e // WG + 1)
                pool.tensor_scalar(w1[:, e, 0, :].rearrange("p (c j) -> p c j", c=NCH),
                                   raw[:, e % RAW, 0, :].rearrange("p (j c) -> p c j", c=NCH),
                                   wscale[:, 0, e:e + 1], 1.0, ALU.mult, ALU.mult).then_inc(whi_pool, 1)
                pool.tensor_scalar(kits[:, e, W2_HI:W2_HI + HID], raw[:, e % RAW, 1, :],
                                   wscale[:, 1, e:e + 1], 1.0, ALU.mult, ALU.mult).then_inc(whi_pool, 1)
            pool.wait_ge(blank_sent, 16)
            pool.wait_ge(rows_done, NG)
            pool.wait_ge(slotrow_done, 1)
            for t in range(NT):
                for k in range(K):
                    pool.indirect_dma_start(slots_dram, bass.IndirectOffsetOnAxis(ap=slotrow[:, k, t:t + 1], axis=0),
                                            rows[:, k, t, :], None).then_inc(rows_sent, 16)
            for n in range(NXG):
                pool.wait_ge(slots_in[n], 16)
            for j in range(TILES):
                pool.wait_ge(y_done, j + 1)
                pool.indirect_dma_start(pairs_dram, bass.IndirectOffsetOnAxis(ap=slots_i[:, j, D:D + 1], axis=0),
                                        ybuf[:, j % NYB, :], None, bounds_check=NT * P * K - 1,
                                        oob_is_err=False).then_inc(y_sent[j % NYB], 16)

        @block.scalar
        def _(act):
            act.dma_start(brb[:, :], br.rearrange("(a e) -> a e", a=1).broadcast_to([P, E])).then_inc(bias_in, 16)
            act.dma_start(bqk[:, 0:1], bq.rearrange("(p a) -> p a", a=1)).then_inc(bias_in, 16)
            act.dma_start(bqk[:, 1:2], bk.rearrange("(p a) -> p a", a=1)).then_inc(bias_in, 16)
            act.dma_start(bvb[:, :], bv.rearrange("(a d) -> a d", a=1).broadcast_to([P, D])).then_inc(bias_in, 16)
            act.dma_start(b1rows[0:E, :], b1).then_inc(bias_in, 16)
            act.dma_start(b1rows[32:32 + E, :], b1).then_inc(bias_in, 16)
            act.dma_start(b1cols[:, :, :], b1.rearrange("e (p c) -> p e c", p=P)).then_inc(bias_in, 16)
            act.dma_start(kits_f[:, :, B2F:B2F + D],
                          b2.rearrange("(a e) d -> a e d", a=1).broadcast_to([P, E, D])).then_inc(b2_in, 16)

            act.wait_ge(wT_done, 1)
            nc.scalar.copy(wqkvT[:, :, :], pO[1][:, 0:3 * D].rearrange("p (n d) -> p n d", n=3)).then_inc(wT_copied, 1)
            act.wait_ge(consts, N_CONST)

            def std_of(g):
                act.wait_ge(var_done, g + 1)
                nc.scalar.activation(std[:, G * g:G * g + G], mv[:, G * g:G * g + G, 1], ACT.Sqrt,
                                     bias=epsc[:, :]).then_inc(std_done, 1)

            def xT_copy(g):
                act.wait_ge(xT_done, g + 1)
                nc.scalar.copy(xT[:, G * P * g:G * P * (g + 1)], pT[g % 2][:, :]).then_inc(xT_copied, 1)

            def rows_hi(g):
                act.wait_ge(xn_done, g + 1)
                nc.scalar.copy(rows[:, 0, G * g:G * g + G, 0:D], xn[:, G * g:G * g + G, :]).then_inc(hi_rows, 1)

            for g in range(NG):
                std_of(g)
                if g:
                    xT_copy(g - 1)
                    rows_hi(g - 1)
            xT_copy(NG - 1)
            rows_hi(NG - 1)

            act.wait_ge(bias_in, 16 * 7)
            for g in range(NG):
                for n, to in enumerate((qT, kT)):
                    act.wait_ge(proj_done, 3 * g + n + 1)
                    nc.scalar.activation(to[:, G * P * g:G * P * (g + 1)], pA(3 * g + n), ACT.Identity,
                                         bias=bqk[:, n:n + 1]).then_inc(proj_copied, 1)
                act.wait_ge(proj_done, 3 * g + 3)
                nc.scalar.copy(v[:, G * g:G * g + G, :],
                               pA(3 * g + 2).rearrange("p (t d) -> p t d", t=G)).then_inc(proj_copied, 1)

            act.wait_ge(gap_done, 1)
            nc.scalar.activation(ex[:, :, :], ex[:, :, :], ACT.Exp)
            nc.scalar.activation(gap[:, :], gap[:, :], ACT.Exp).then_inc(ex_done, 1)

            def squares(e):
                act.wait_ge(w_in[e // 2], 32)
                nc.scalar.activation(w1[:, e, 1, :], raw[:, e % RAW, 0, :], ACT.Square,
                                     accum_out=sumsq[:, 0, e:e + 1]).then_inc(sq_done, 1)
                nc.scalar.activation(kits[:, e, W2_LO:W2_LO + HID], raw[:, e % RAW, 1, :], ACT.Square,
                                     accum_out=sumsq[:, 2, e:e + 1]).then_inc(sq_done, 1)

            def high(e):
                act.wait_ge(scale_done, e // WG + 1)
                nc.scalar.activation(w1[:, e, 0, :].rearrange("p (c j) -> p c j", c=NCH),
                                     raw[:, e % RAW, 0, :].rearrange("p (j c) -> p c j", c=NCH),
                                     ACT.Copy, scale=wscale[:, 0, e:e + 1]).then_inc(whi_act, 1)
                nc.scalar.activation(kits[:, e, W2_HI:W2_HI + HID], raw[:, e % RAW, 1, :],
                                     ACT.Copy, scale=wscale[:, 1, e:e + 1]).then_inc(whi_act, 1)

            def softmax(t):
                n = (t % TB + 1) * P
                act.wait_ge(max_done, t + 1)
                if t >= 2:
                    act.wait_ge(pt_done, groups_until(t - 1))
                nc.scalar.activation(probs[:, t % 2, 0:n], pS[t % 2][:, 0:n], ACT.Exp, bias=negm[:, t:t + 1],
                                     scale=SCALE, accum_out=rsum[:, t:t + 1]).then_inc(exp_done, 1)

            def probsT_copy(t):
                u = groups_until(t)
                n = min(t % TB + 1, G) * P
                act.wait_ge(pt_done, u + 1)
                if t >= 1:
                    act.wait_ge(o_done, t)
                nc.scalar.copy(probsT[:, 0, 0:n], pT[0][:, 0:n]).then_inc(pt_act, 1)

            for t in range(NT):
                softmax(t)
                squares(t)
                probsT_copy(t)
                if t - WG >= POOL_HI:
                    high(t - WG)
            for e in range(NT - WG, NT):
                high(e)

            def xs_copy(j):
                act.wait_ge(xs_done, j + 1)
                if j >= 3:
                    act.wait_ge(l1_done, j - 2)
                nc.scalar.copy(xslot[:, j % 3, :], pT[j % 2][:, :].bitcast(F16)[:, 0:2 * D]).then_inc(xs_copied, 1)

            xs_copy(0)
            xs_copy(1)
            for j in range(TILES):
                act.wait_ge(l1_done, j + 1)
                if j >= NHB:
                    act.wait_ge(l2_done, j - NHB + 1)
                nc.scalar.activation(hid[:, j % NHB, 0, :], pA(j % 2), ACT.Relu).then_inc(hi_done, 1)
                if j + 2 < TILES:
                    xs_copy(j + 2)

        @block.vector
        def _(dve):
            made = [0]

            def step(ins):
                made[0] += 1
                ins.then_inc(dve_step, 1)
                dve.wait_ge(dve_step, made[0])

            def moments(g):
                dve.wait_ge(x_in[g], 16)
                for t in range(G * g, G * g + G):
                    ins = dve.bn_stats(stats[:, t, :], xin[:, t, :])
                step(ins)
                for t in range(G * g, G * g + G):
                    ins = dve.bn_aggr(mv[:, t, :], stats[:, t, :])
                ins.then_inc(var_done, 1)

            def normalise(g):
                dve.wait_ge(std_done, g + 1)
                step(dve.reciprocal(rstd[:, G * g:G * g + G], std[:, G * g:G * g + G]))
                for t in range(G * g, G * g + G):
                    ins = dve.tensor_scalar(xn[:, t, :], xin[:, t, :], mv[:, t, 0:1], rstd[:, t:t + 1],
                                            ALU.subtract, ALU.mult)
                ins.then_inc(xn_done, 1)

            def rows_lo(g):
                dve.wait_ge(hi_rows, g + 1)
                step(dve.tensor_tensor(rows[:, 0, G * g:G * g + G, D:2 * D], xn[:, G * g:G * g + G, :],
                                       rows[:, 0, G * g:G * g + G, 0:D], ALU.subtract))
                dve.tensor_copy(rows[:, 1, G * g:G * g + G, 0:2 * D],
                                rows[:, 0, G * g:G * g + G, 0:2 * D]).then_inc(rows_done, 1)

            moments(0)
            for g in range(NG):
                if g + 1 < NG:
                    moments(g + 1)
                normalise(g)
                if g:
                    rows_lo(g - 1)
            rows_lo(NG - 1)

            dve.wait_ge(bias_in, 16 * 7)
            dve.wait_ge(consts, N_CONST)
            dve.wait_ge(logits_done, NG)

            def over_tiles(a):
                return a[:, :, None].broadcast_to([P, E, NT])

            def over_experts(a):
                return a[:, None, :].broadcast_to([P, E, NT])

            def by_token(a):
                return a.rearrange("p e t -> p t e")

            step(dve.tensor_tensor(lg[:, :, :], pO[0][:, 0:NT * E].rearrange("p (t e) -> p e t", e=E),
                                   over_tiles(brb[:, :]), ALU.add))
            step(dve.tensor_reduce(best[:, 0, :], by_token(lg[:, :, :]), AX.X, ALU.max))
            for k, logits in enumerate((lg, lg2)):
                step(dve.tensor_tensor(hit[:, :, :], logits[:, :, :], over_experts(best[:, k, :]), ALU.is_equal))
                step(dve.tensor_tensor(hit[:, :, :], hit[:, :, :], rev[:, :, :], ALU.mult))
                step(dve.tensor_reduce(pick[:, :], by_token(hit[:, :, :]), AX.X, ALU.max))
                step(dve.tensor_tensor(oh[:, k, :, :], rev[:, :, :], over_experts(pick[:, :]), ALU.is_equal))
                if k == 0:
                    step(dve.scalar_tensor_tensor(out=lg2[:, :, :], in0=oh[:, 0, :, :], scalar=-HUGE,
                                                  in1=lg[:, :, :], op0=ALU.mult, op1=ALU.add))
                    step(dve.tensor_reduce(best[:, 1, :], by_token(lg2[:, :, :]), AX.X, ALU.max))
            dve.tensor_tensor(chosen[:, :, :], oh[:, 0, :, :], oh[:, 1, :, :], ALU.add).then_inc(chosen_done, 1)
            dve.tensor_tensor(ex[:, :, :], lg[:, :, :], over_experts(best[:, 0, :]), ALU.subtract)
            dve.tensor_tensor(gap[:, :], best[:, 1, :], best[:, 0, :], ALU.subtract).then_inc(gap_done, 1)

            dve.wait_ge(ranks_done, 1)
            rank = pO[0][:, 0:E * NT]
            total = pO[0][:, E * NT:2 * E * NT]

            def flat(a):
                return a.rearrange("p e t -> p (e t)")

            step(dve.tensor_tensor_scan(flat(incl[:, :, :]), flat(keep[:, :, :]), total, 0.0, ALU.mult, ALU.add))
            step(dve.tensor_tensor(flat(pos[:, :, :]), flat(incl[:, :, :]), total, ALU.subtract))
            step(dve.tensor_tensor(flat(pos[:, :, :]), flat(pos[:, :, :]), rank, ALU.add))
            step(dve.tensor_scalar(cnt[:, :], incl[:, :, NT - 1], float(P - 1), None, ALU.add))
            step(dve.tensor_scalar(ntile[:, :], cnt[:, :], P.bit_length() - 1, None, ALU.logical_shift_right))
            step(dve.tensor_copy(ntilef[:, :], ntile[:, :]))
            step(dve.tensor_tensor_scan(cum[:, :], ones[:, 0:E], ntilef[:, :], 0.0, ALU.mult, ALU.add))
            step(dve.tensor_tensor(start[:, :], cum[:, :], ntilef[:, :], ALU.subtract))
            step(dve.scalar_tensor_tensor(out=pos[:, :, :], in0=over_tiles(start[:, :]), scalar=float(P),
                                          in1=pos[:, :, :], op0=ALU.mult, op1=ALU.add))
            for k in range(K):
                step(dve.tensor_tensor(hit[:, :, :], oh[:, k, :, :], pos[:, :, :], ALU.mult))
                step(dve.tensor_reduce(posk[:, k, :], by_token(hit[:, :, :]), AX.X, ALU.add))
            step(dve.tensor_copy(posi[:, :, :], posk[:, :, :]))
            dve.tensor_scalar(posr[:, :, :], posi[:, :, :], P.bit_length() - 1, None, ALU.logical_shift_right)
            step(dve.tensor_scalar(posi[:, :, :], posi[:, :, :], P - 1, None, ALU.bitwise_and))
            dve.scalar_tensor_tensor(out=slotrow[:, :, :], in0=posi[:, :, :], scalar=float(TILES),
                                     in1=posr[:, :, :], op0=ALU.mult, op1=ALU.add).then_inc(slotrow_done, 1)
            step(dve.tensor_tensor(past[:, :, :], cum[0:1, None, :].broadcast_to([1, TILES + 1, E]),
                                   tileno[0:1, :, None].broadcast_to([1, TILES + 1, E]), ALU.is_le))
            step(dve.tensor_reduce(expertf[:, :], past[:, :, :], AX.X, ALU.add))
            dve.tensor_scalar(expert[:, :], expertf[:, :], float(E - 1), None, ALU.min).then_inc(expert_done, 1)

            dve.wait_ge(ex_done, 1)
            step(dve.tensor_reduce(exsum[:, :], by_token(ex[:, :, :]), AX.X, ALU.add))
            step(dve.reciprocal(gate[:, 0, :], exsum[:, :]))
            dve.tensor_tensor(gate[:, 1, :], gate[:, 0, :], gap[:, :], ALU.mult)
            step(dve.tensor_tensor(b1sq[:, :, :], b1cols[:, :, :], b1cols[:, :, :], ALU.mult))
            step(dve.tensor_reduce(sumsq[:, 1, :], b1sq[:, :, :], AX.X, ALU.add))

            def scales(g):
                s = slice(WG * g, WG * g + WG)
                dve.wait_ge(sums_done, g + 1)
                step(dve.tensor_scalar(nrm[:, :, s], pO[1][:, 0:3 * WG].rearrange("p (n e) -> p n e", n=3),
                                       2.0 ** -120, None, ALU.max))
                step(dve.tensor_scalar(nrmi[:, :, s], nrm[:, :, s].bitcast(I32), 23, None,
                                       ALU.logical_shift_right))
                step(dve.tensor_scalar(nrmi2[:, :, s], nrmi[:, :, s], 127.0, None, ALU.add))
                step(dve.tensor_scalar(pw[:, :, s], nrmi2[:, :, s], 1, 23, ALU.logical_shift_right,
                                       ALU.logical_shift_left))
                step(dve.scalar_tensor_tensor(out=bound[:, s], in0=pw[:, 0, s].bitcast(F32), scalar=16.0,
                                              in1=pw[:, 1, s].bitcast(F32), op0=ALU.mult, op1=ALU.add))
                dve.tensor_copy(pb[:, 1, s], pw[:, 2, s])
                step(dve.tensor_scalar(pb[:, 0, s], bound[:, s].bitcast(I32), 0x7F800000, None, ALU.bitwise_and))
                step(dve.reciprocal(inv[:, :, s], pb[:, :, s].bitcast(F32)))
                dve.scalar_tensor_tensor(out=kits_f[:, s, CF], in0=pb[:, 0, s].bitcast(F32), scalar=2.0 ** -26,
                                         in1=pb[:, 1, s].bitcast(F32), op0=ALU.mult, op1=ALU.mult)
                dve.tensor_scalar(wscale[:, :, s], inv[:, :, s], 2.0 ** 13, None, ALU.mult).then_inc(scale_done, 1)

            def low(e):
                if e < POOL_HI:
                    dve.wait_ge(whi_pool, 2 * e + 2)
                else:
                    dve.wait_ge(whi_act, 2 * (e - POOL_HI) + 2)
                dve.wait_ge(scale_done, e // WG + 1)
                dve.scalar_tensor_tensor(out=w1[:, e, 1, :].rearrange("p (c j) -> p c j", c=NCH),
                                         in0=raw[:, e % RAW, 0, :].rearrange("p (j c) -> p c j", c=NCH),
                                         scalar=wscale[:, 0, e:e + 1],
                                         in1=w1[:, e, 0, :].rearrange("p (c j) -> p c j", c=NCH),
                                         op0=ALU.mult, op1=ALU.subtract).then_inc(wlo_done, 1)
                dve.scalar_tensor_tensor(out=kits[:, e, W2_LO:W2_LO + HID], in0=raw[:, e % RAW, 1, :],
                                         scalar=wscale[:, 1, e:e + 1], in1=kits[:, e, W2_HI:W2_HI + HID],
                                         op0=ALU.mult, op1=ALU.subtract).then_inc(wlo_done, 1)

            def row_max(t):
                i = t % TB
                sc = pS[t % 2]
                dve.wait_ge(s_done, t + 1)
                if i:
                    step(dve.tensor_reduce(m0[:, t:t + 1], sc[:, 0:i * P], AX.X, ALU.max))
                step(dve.tensor_tensor_reduce(out=sc[:, i * P:(i + 1) * P], in0=sc[:, i * P:(i + 1) * P],
                                              in1=causal[:, :], scale=1.0, scalar=m0[:, t:t + 1] if i else -HUGE,
                                              op0=ALU.add, op1=ALU.max, accum_out=m1[:, t:t + 1]))
                dve.tensor_scalar(negm[:, t:t + 1], m1[:, t:t + 1], -SCALE, None, ALU.mult).then_inc(max_done, 1)

            def probsT_copy(t):
                if t % TB + 1 > G:
                    n = (t % TB + 1 - G) * P
                    dve.wait_ge(pt_done, groups_until(t) + 2)
                    if t >= 1:
                        dve.wait_ge(o_done, t)
                    dve.tensor_copy(probsT[:, 1, 0:n], pT[1][:, 0:n]).then_inc(pt_dve, 1)

            def attended(t):
                dve.wait_ge(exp_done, t + 1)
                step(dve.reciprocal(rinv[:, t:t + 1], rsum[:, t:t + 1]))
                dve.wait_ge(o_done, t + 1)
                dve.wait_ge(xbv_done, t + 1)
                dve.scalar_tensor_tensor(out=xin[:, t, :], in0=pO[0][:, 0:D], scalar=rinv[:, t:t + 1],
                                         in1=xin[:, t, :], op0=ALU.mult, op1=ALU.add).then_inc(o_read, 1)

            row_max(0)
            for t in range(NT):
                if t + 1 < NT:
                    row_max(t + 1)
                probsT_copy(t)
                attended(t)
                if t % WG == WG - 1:
                    scales(t // WG)
                if t >= WG:
                    low(t - WG)
            for e in range(NT - WG, NT):
                low(e)
            hi_b, lo_b = b1parts[0:E, :], b1parts[32:32 + E, :]
            for at in (0, 32):
                dve.tensor_tensor(b1tmp[at:at + E, :], wscale[at:at + E, 0, :], ident[at:at + E, at:at + E], ALU.mult)
            step(dve.memset(b1s[:, :], 0.0))
            for at in (0, 32):
                ins = dve.tensor_reduce(b1s[at:at + E, :], b1tmp[at:at + E, :], AX.X, ALU.add)
            step(ins)
            for at in (0, 32):
                ins = dve.tensor_scalar(b1rows[at:at + E, :], b1rows[at:at + E, :], b1s[at:at + E, :], None, ALU.mult)
            step(ins)
            step(dve.tensor_copy(hi_b, b1rows[0:E, :]))
            step(dve.tensor_copy(lo_b, b1rows[32:32 + E, :]))
            step(dve.tensor_tensor(b1rows[32:32 + E, :], b1rows[32:32 + E, :], lo_b, ALU.subtract))
            dve.tensor_copy(lo_b, b1rows[32:32 + E, :]).then_inc(b1_done, 1)

            def y_of(j):
                dve.wait_ge(l2_done, j + 1)
                dve.wait_ge(staged[j % NST], 16 * (j // NST + 1))
                if j >= NYB:
                    dve.wait_ge(y_sent[j % NYB], 16 * (j // NYB))
                dve.scalar_tensor_tensor(out=ybuf[:, j % NYB, :], in0=pO[j % 2][:, 0:D],
                                         scalar=stage_f[:, j % NST, CF:CF + 1],
                                         in1=stage_f[:, j % NST, B2F:B2F + D],
                                         op0=ALU.mult, op1=ALU.add).then_inc(y_done, 1)

            for j in range(TILES):
                dve.wait_ge(hi_done, j + 1)
                dve.scalar_tensor_tensor(out=hid[:, j % NHB, 1, :], in0=pA(j % 2), scalar=0.0,
                                         in1=hid[:, j % NHB, 0, :], op0=ALU.max,
                                         op1=ALU.subtract).then_inc(lo_done, 1)
                if j >= 2:
                    y_of(j - 2)
            y_of(TILES - 2)
            y_of(TILES - 1)

            for n in range(NYL):
                dve.wait_ge(pairs_in[n], 16)
                for k in range(K):
                    for t in range(TYL * n, TYL * n + TYL):
                        ins = dve.scalar_tensor_tensor(out=xin[:, t, :], in0=pairs[:, t, k, :],
                                                       scalar=gate[:, k, t:t + 1], in1=xin[:, t, :],
                                                       op0=ALU.mult, op1=ALU.add)
                    if k == 0:
                        step(ins)
                ins.then_inc(res_done, 1)

        @block.tensor
        def _(pe):
            pe.wait_ge(consts, N_CONST)
            pe.wait_ge(small_in, 16 * 4)
            for n in range(3):
                ins = pe.transpose(pO[1][:, n * D:(n + 1) * D], wqkv[:, n, :], ident[:, :])
            ins.then_inc(wT_done, 1)

            def x_transposes(g):
                pe.wait_ge(xn_done, g + 1)
                if g >= 2:
                    pe.wait_ge(xT_copied, g - 1)
                for i in range(G):
                    ins = pe.transpose(pT[g % 2][:, i * P:(i + 1) * P], xn[:, G * g + i, :], ident[:, :])
                ins.then_inc(xT_done, 1)

            def router(g):
                pe.wait_ge(xT_copied, g + 1)
                for t in range(G * g, G * g + G):
                    ins = pe.matmul(pO[0][:, t * E:(t + 1) * E], xT[:, t * P:(t + 1) * P], wr[:, :],
                                    start=True, stop=True)
                ins.then_inc(logits_done, 1)

            for g in range(NG):
                x_transposes(g)
                if g:
                    router(g - 1)
            router(NG - 1)

            pe.wait_ge(wT_copied, 1)
            for g in range(NG):
                cols = slice(G * P * g, G * P * (g + 1))
                for n in range(3):
                    if 3 * g + n >= 4:
                        pe.wait_ge(proj_copied, 3 * g + n - 3)
                    if n < 2:
                        ins = pe.matmul(pA(3 * g + n), wqkvT[:, n, :], xT[:, cols], start=True, stop=True)
                    else:
                        for i in range(G):
                            t = G * g + i
                            ins = pe.matmul(pA(3 * g + 2)[:, i * D:(i + 1) * D], xT[:, t * P:(t + 1) * P],
                                            wqkvT[:, 2, :], start=True, stop=True)
                    ins.then_inc(proj_done, 1)
                if g == 1:
                    pe.wait_ge(chosen_done, 1)
                    m = chosen[:, :, :].rearrange("p e t -> p (e t)")
                    pe.matmul(pO[0][:, 0:E * NT], before[:, :], m, start=True, stop=True)
                    pe.matmul(pO[0][:, E * NT:2 * E * NT], ones16[:, :], m, start=True,
                              stop=True).then_inc(ranks_done, 1)

            def scores(t):
                n = (t % TB + 1) * P
                if t >= 2:
                    pe.wait_ge(exp_done, t - 1)
                if t == 0:
                    pe.wait_ge(proj_copied, 3 * NG)
                at = t // TB * S
                for a in range(0, n, 512):
                    z = min(a + 512, n)
                    ins = pe.matmul(pS[t % 2][:, a:z], qT[:, t * P:(t + 1) * P], kT[:, at + a:at + z],
                                    start=True, stop=True)
                ins.then_inc(s_done, 1)

            def probs_transposes(t):
                pe.wait_ge(exp_done, t + 1)
                if t >= 1:
                    pe.wait_ge(pt_act, t)
                    second = sum(u % TB + 1 > G for u in range(t))
                    if second:
                        pe.wait_ge(pt_dve, second)
                for a in range(0, t % TB + 1, G):
                    for j in range(a, min(a + G, t % TB + 1)):
                        ins = pe.transpose(pT[a // G][:, (j - a) * P:(j - a + 1) * P],
                                           probs[:, t % 2, j * P:(j + 1) * P], ident[:, :])
                    ins.then_inc(pt_done, 1)

            def attend(t):
                i = t % TB
                pe.wait_ge(pt_act, t + 1)
                if i + 1 > G:
                    pe.wait_ge(pt_dve, sum(u % TB + 1 > G for u in range(t + 1)))
                if t:
                    pe.wait_ge(o_read, t)
                else:
                    pe.wait_ge(slotrow_done, 1)
                for j in range(i + 1):
                    ins = pe.matmul(pO[0][:, 0:D], probsT[:, j // G, j % G * P:(j % G + 1) * P],
                                    v[:, t // TB * TB + j, :], start=(j == 0), stop=(j == i))
                ins.then_inc(o_done, 1)

            def weight_sums(g):
                pe.wait_ge(sq_done, 2 * WG * (g + 1))
                pe.wait_ge(gap_done, 1)
                if g:
                    pe.wait_ge(scale_done, g)
                for n in range(3):
                    ins = pe.matmul(pO[1][:, n * WG:(n + 1) * WG], ones[:, :], sumsq[:, n, WG * g:WG * g + WG],
                                    start=True, stop=True)
                ins.then_inc(sums_done, 1)

            scores(0)
            scores(1)
            for t in range(NT):
                probs_transposes(t)
                if t + 2 < NT:
                    scores(t + 2)
                attend(t)
                if t % WG == WG - 1:
                    weight_sums(t // WG)

            def slot_transposes(j):
                pe.wait_ge(slots_in[j // XG], 16)
                if j >= 2:
                    pe.wait_ge(xs_copied, j - 1)
                else:
                    pe.wait_ge(pt_act, NT)
                to = pT[j % 2][:, :].bitcast(F16)
                pe.transpose(to[:, 0:D], slots[:, j, 0:D], ident16[:, :])
                pe.transpose(to[:, D:2 * D], slots[:, j, D:2 * D], ident16[:, :]).then_inc(xs_done, 1)

            def hidden_and_result(j, r):
                def second(c):
                    if r is None:
                        return None
                    s = stage[:, r % NST, :]
                    hb = hid[:, r % NHB]
                    y = pO[r % 2][:, 0:D]
                    h_hi, h_lo = hb[:, 0, c * P:(c + 1) * P], hb[:, 1, c * P:(c + 1) * P]
                    w_hi = s[:, W2_HI + c * P:W2_HI + (c + 1) * P]
                    w_lo = s[:, W2_LO + c * P:W2_LO + (c + 1) * P]
                    pe.matmul(y, h_hi, w_hi, start=(c == 0), stop=False)
                    pe.matmul(y, h_hi, w_lo, start=False, stop=False)
                    return pe.matmul(y, h_lo, w_hi, start=False, stop=(c == NCH - 1))

                if r is not None:
                    pe.wait_ge(lo_done, r + 1)
                    pe.wait_ge(staged[r % NST], 16 * (r // NST + 1))
                    if r >= 2:
                        pe.wait_ge(y_done, r - 1)
                if j is None:
                    for c in range(NCH):
                        ins = second(c)
                    ins.then_inc(l2_done, 1)
                    return
                e = nc.s_assert_within(
                    pe.value_load(expert[0:1, j:j + 1]), 0, E - 1,
                    skip_runtime_bounds_check_because="a count of experts, held to E - 1 by a min")
                pe.wait_ge(xs_copied, j + 1)
                pe.wait_ge(staged[j % NST], 16 * (j // NST + 1))
                if j >= 2:
                    pe.wait_ge(lo_done, j - 1)
                bank = pA(j % 2)
                x_hi, x_lo = xslot[:, j % 3, 0:D], xslot[:, j % 3, D:2 * D]
                for c in range(NCH):
                    pe.matmul(bank[:, c * P:(c + 1) * P], b1parts[:, c:HID:NCH],
                              stage[:, j % NST, SEL:SEL + P], start=(c == 0), stop=False, skip_group_check=True)
                for c in range(NCH):
                    to = bank[:, c * P:(c + 1) * P]
                    w_hi = w1[:, bass.ds(e, 1), 0, c * P:(c + 1) * P].rearrange("p a h -> p (a h)")
                    pe.matmul(to, w_hi, x_hi, start=False, stop=False, skip_group_check=True)
                    pe.matmul(to, w_hi, x_lo, start=False, stop=False, skip_group_check=True)
                    last2 = second(c)
                    w_lo = w1[:, bass.ds(e, 1), 1, c * P:(c + 1) * P].rearrange("p a h -> p (a h)")
                    ins = pe.matmul(to, w_lo, x_hi, start=False, stop=(c == NCH - 1), skip_group_check=True)
                if last2 is not None:
                    last2.then_inc(l2_done, 1)
                ins.then_inc(l1_done, 1)

            slot_transposes(0)
            slot_transposes(1)
            pe.wait_ge(expert_done, 1)
            pe.wait_ge(wlo_done, 2 * E)
            pe.wait_ge(b1_done, 1)
            pe.wait_ge(o_read, NT)
            for j in range(TILES):
                hidden_and_result(j, j - 2 if j >= 2 else None)
                if j + 2 < TILES:
                    slot_transposes(j + 2)
            hidden_and_result(None, TILES - 2)
            hidden_and_result(None, TILES - 1)


_INS = ["L0_attn_x", "L0_attn_Wk", "L0_attn_bk", "L0_attn_Wq", "L0_attn_bq", "L0_attn_Wv", "L0_attn_bv",
        "L0_ffn_Wr", "L0_ffn_br", "L0_ffn_W1", "L0_ffn_b1", "L0_ffn_W2", "L0_ffn_b2"]


def kernel(**inputs):
    import numpy as np
    import concourse.bacc as bacc
    from concourse import mybir as mb
    from concourse.bass_utils import run_bass_kernel_spmd

    nc = bacc.Bacc("TRN2", target_bir_lowering=False, num_devices=1)
    arrays, args = {}, []
    for name in _INS:
        a = np.ascontiguousarray(inputs[name])
        arrays[f"in_{name}"] = a
        args.append(nc.dram_tensor(f"in_{name}", a.shape, mb.dt.from_np(a.dtype), kind="ExternalInput").ap())
    out = nc.dram_tensor("out_0", inputs["L0_attn_x"].shape, F32, kind="ExternalOutput").ap()
    attention_and_top2_experts(nc, *args, out)
    r = run_bass_kernel_spmd(nc, [arrays], core_ids=[0])
    return r.results[0]["out_0"]
```

```python
from contextlib import ExitStack

import concourse.bass as bass
from concourse import mybir

ALU = mybir.AluOpType
ACT = mybir.ActivationFunctionType
AX = mybir.AxisListType
F32 = mybir.dt.float32
F16 = mybir.dt.float16
I32 = mybir.dt.int32

P = 128
HUGE = 3.0e38


def attention_and_top2_experts(nc, x, Wk, bk, Wq, bq, Wv, bv, Wr, br, W1, b1, W2, b2, out):
    B, S, D = x.shape
    E = Wr.shape[1]
    HID = W1.shape[2]
    K = 2
    NT = B * S // P
    TB = S // P
    NCH = HID // P
    TILES = K * NT + E - 1
    EPS = 1e-5
    SCALE = float(D) ** -0.5
    G = 4
    NG = NT // G
    assert D == P and HID == NCH * P

    ROW = 2 * D + 4
    W1_HI, W1_LO, KIT_AT = 0, HID, 2 * HID
    W2_HI, W2_LO, SEL, B2F = 0, HID, 2 * HID, (2 * HID + P) // 2
    CF = B2F + D
    KIT = 2 * (CF + 1)
    EW = KIT_AT + KIT
    RAW = 6
    WG = 2
    NST, NHB, NYB = 6, 3, 4
    XG = 12
    NXG = -(-TILES // XG)
    NYL = 4
    LEAD = 4
    TYL = NT // NYL

    slots_dram = nc.dram_tensor("slots_dram", (P * TILES, ROW), F16).ap()
    pairs_dram = nc.dram_tensor("pairs_dram", (NT * P * K, D), F32).ap()

    with ExitStack() as ctx:
        def sb(name, shape, dt):
            return ctx.enter_context(nc.sbuf_tensor(name, shape, dt))

        def sem(name):
            return ctx.enter_context(nc.semaphore(name))

        xin = sb("xin", [P, NT, D], F32)
        xn = sb("xn", [P, NT, D], F32)
        xT = sb("xT", [P, NT * P], F32)
        qT = sb("qT", [P, NT * P], F32)
        kT = sb("kT", [P, NT * P], F32)
        v = sb("v", [P, NT, D], F32)
        wts = sb("wts", [P, E, EW], F16)
        raw = sb("raw", [P, RAW, 2, HID], F32)
        probsT = sb("probsT", [P, 2, G * P], F32)
        wr = sb("wr", [P, E], F32)
        brb = sb("brb", [P, E], F32)
        bqk = sb("bqk", [P, 2], F32)
        bvb = sb("bvb", [P, D], F32)
        b1rows = sb("b1rows", [P, HID], F32)
        b1parts = sb("b1parts", [P, HID], F16)
        stats = sb("stats", [P, NT, 6], F32)
        mv = sb("mv", [P, NT, 2], F32)
        std = sb("std", [P, NT], F32)
        rstd = sb("rstd", [P, NT], F32)
        epsc = sb("epsc", [P, 1], F32)
        ident = sb("ident", [P, P], F32)
        ident16 = sb("ident16", [P, P], F16)
        causal = sb("causal", [P, P], F32)
        before = sb("before", [P, P], F16)
        ones16 = sb("ones16", [P, P], F16)
        ones = sb("ones", [P, P], F32)
        tileno = sb("tileno", [P, TILES + 1], F32)
        scratch_i = sb("scratch_i", [P, TILES + 1], I32)
        blank = sb("blank", [P, ROW], F16)
        chosen = sb("chosen", [P, E, NT], F16)
        best = sb("best", [P, K, NT], F32)
        pick = sb("pick", [P, NT], F32)
        exsum = sb("exsum", [P, NT], F32)
        gap = sb("gap", [P, NT], F32)
        gate = sb("gate", [P, K, NT], F32)
        posk = sb("posk", [P, K, NT], F32)
        posi = sb("posi", [P, K, NT], I32)
        posr = sb("posr", [P, K, NT], I32)
        slotrow = sb("slotrow", [P, K, NT], I32)
        cnt = sb("cnt", [P, E], I32)
        ntile = sb("ntile", [P, E], I32)
        ntilef = sb("ntilef", [P, E], F32)
        cum = sb("cum", [P, E], F32)
        start = sb("start", [P, E], F32)
        expertf = sb("expertf", [1, TILES + 1], F32)
        expert = sb("expert", [1, TILES + 1], I32)
        sumsq = sb("sumsq", [P, E], F32)
        b1sum = sb("b1sum", [P, E], F32)
        nrm = sb("nrm", [P, E], F32)
        expo = sb("expo", [P, E], I32)
        expo2 = sb("expo2", [P, E], I32)
        pw = sb("pw", [P, E], I32)
        inv = sb("inv", [P, E], F32)
        wscale = sb("wscale", [P, E], F32)
        b1s = sb("b1s", [P, 1], F32)
        b1tmp = sb("b1tmp", [P, E], F32)
        m0 = sb("m0", [P, NT], F32)
        m1 = sb("m1", [P, NT], F32)
        negm = sb("negm", [P, NT], F32)
        rsum = sb("rsum", [P, NT], F32)
        rinv = sb("rinv", [P, NT], F32)

        slot_space = sb("slot_space", [P, TILES * ROW], F16)
        slots = slot_space[:, :].rearrange("p (t c) -> p t c", t=TILES)
        rows = slot_space[:, 0:K * NT * ROW].rearrange("p (k t c) -> p k t c", k=K, t=NT)

        stage_w, hid_w, xslot_w, ybuf_w = NST * KIT, NHB * 2 * HID, 3 * 2 * D, NYB * 2 * D
        space = sb("space", [P, stage_w + ybuf_w], F16)
        stage = space[:, 0:stage_w].rearrange("p (s c) -> p s c", s=NST)
        ybuf = space[:, stage_w:stage_w + ybuf_w].bitcast(F32).rearrange("p (s d) -> p s d", s=NYB)

        taken = [0]

        def early(n, parts=P):
            a = 2 * taken[0]
            taken[0] += n
            assert 2 * taken[0] <= stage_w + ybuf_w
            return space[0:parts, a:a + 2 * n].bitcast(F32)

        def per_expert(n=1):
            return early(n * E * NT).rearrange("p (e t) -> p e t", t=NT)

        wqkv = early(3 * D).rearrange("p (n d) -> p n d", n=3)
        wqkvT = early(3 * D).rearrange("p (n d) -> p n d", n=3)
        b1cols = early(E * NCH).rearrange("p (e c) -> p e c", e=E)
        b1sq = early(E * NCH).rearrange("p (e c) -> p e c", e=E)
        rev, keep = per_expert(), per_expert()
        lg, lg2, hit, ex, incl, pos = (per_expert() for _ in range(6))
        oh = early(K * E * NT).rearrange("p (k e t) -> p k e t", k=K, e=E)
        past = early((TILES + 1) * E, 1).rearrange("p (t e) -> p t e", e=E)

        hid = xT[:, 0:hid_w // 2].bitcast(F16).rearrange("p (s a h) -> p s a h", s=NHB, a=2)
        xslot = xT[:, hid_w // 2:(hid_w + xslot_w) // 2].bitcast(F16).rearrange("p (s c) -> p s c", s=3)

        probs = xn[:, :, :].rearrange("p t d -> p (t d)").rearrange("p (a n) -> p a n", a=2)
        pairs = raw[:, 0:4, :, :].rearrange("p r w h -> p (r w h)").rearrange(
            "p (t k d) -> p t k d", k=K, d=D)
        slots_i = slot_space[:, :].bitcast(I32).rearrange(
            "p (t c) -> p t c", t=TILES)
        rows_i = slot_space[:, 0:K * NT * ROW].bitcast(I32).rearrange(
            "p (k t c) -> p k t c", k=K, t=NT)
        wts_f = wts[:, :, :].rearrange("p e c -> p (e c)").bitcast(F32).rearrange("p (e c) -> p e c", e=E)
        stage_f = space[:, 0:stage_w].bitcast(F32).rearrange(
            "p (s c) -> p s c", s=NST)

        wts_i = wts[:, :, :].rearrange("p e c -> p (e c)").bitcast(I32).rearrange("p (e c) -> p e c", e=E)
        stage_i = space[:, 0:stage_w].bitcast(I32).rearrange("p (s c) -> p s c", s=NST)

        pS = [ctx.enter_context(nc.psum_tensor(f"pS{n}", [P, 1024], F32)) for n in range(2)]
        pT = [ctx.enter_context(nc.psum_tensor(f"pT{n}", [P, 512], F32)) for n in range(2)]
        pO = [ctx.enter_context(nc.psum_tensor(f"pO{n}", [P, 512], F32)) for n in range(2)]

        def pA(n):
            return pS[n % 4 // 2][:, 512 * (n % 2):512 * (n % 2) + 512]

        x_in = [sem(f"x_in{g}") for g in range(NG)]
        bias_in = sem("bias_in")
        b2_in = sem("b2_in")
        w_in = [sem(f"w_in{n}") for n in range(E // 2)]
        blank_sent = sem("blank_sent")
        rows_sent = sem("rows_sent")
        slots_in = [sem(f"slots_in{n}") for n in range(NXG)]
        staged = [sem(f"staged{n}") for n in range(NST)]
        y_sent = [sem(f"y_sent{n}") for n in range(NYB)]
        pairs_in = [sem(f"pairs_in{n}") for n in range(NYL)]
        out_sent = sem("out_sent")
        ident_made = sem("ident_made")
        blank_made = sem("blank_made")
        consts = sem("consts")
        pool_step = sem("pool_step")
        dve_step = sem("dve_step")
        wT_done = sem("wT_done")
        wT_copied = sem("wT_copied")
        var_done = sem("var_done")
        std_done = sem("std_done")
        xn_done = sem("xn_done")
        xT_done = sem("xT_done")
        xT_copied = sem("xT_copied")
        hi_rows = sem("hi_rows")
        rows_done = sem("rows_done")
        logits_done = sem("logits_done")
        chosen_done = sem("chosen_done")
        ranks_done = sem("ranks_done")
        slotrow_done = sem("slotrow_done")
        expert_done = sem("expert_done")
        gap_done = sem("gap_done")
        ex_done = sem("ex_done")
        proj_done = sem("proj_done")
        proj_copied = sem("proj_copied")
        xbv_done = sem("xbv_done")
        sq_done = sem("sq_done")
        b1sum_done = sem("b1sum_done")
        sums_done = sem("sums_done")
        scale_done = sem("scale_done")
        whi_done = sem("whi_done")
        wlo_done = sem("wlo_done")
        b1_done = sem("b1_done")
        s_done = sem("s_done")
        max_done = sem("max_done")
        exp_done = sem("exp_done")
        pt_done = sem("pt_done")
        pt_act = sem("pt_act")
        pt_dve = sem("pt_dve")
        o_done = sem("o_done")
        o_read = sem("o_read")
        xs_done = sem("xs_done")
        xs_copied = sem("xs_copied")
        l1_done = sem("l1_done")
        hi_done = sem("hi_done")
        lo_done = sem("lo_done")
        l2_done = sem("l2_done")
        y_done = sem("y_done")
        res_done = sem("res_done")

        x_v = x.rearrange("b (t p) d -> p (b t) d", p=P)
        out_v = out.rearrange("b (t p) d -> p (b t) d", p=P)
        slots_v = slots_dram.rearrange("(p t) c -> p t c", p=P)
        pairs_v = pairs_dram.rearrange("(t p k) d -> p t k d", p=P, k=K)
        w1_v = W1.rearrange("e d h -> d e h")
        w2_v = W2.rearrange("e (p c) m -> p e (c m)", p=P)

        def high_part(e):
            return wts[:, e, 0:4 * HID].rearrange("p (w a h) -> p w a h", w=2, a=2)[:, :, 0, :]

        def low_part(e):
            return wts[:, e, 0:4 * HID].rearrange("p (w a h) -> p w a h", w=2, a=2)[:, :, 1, :]

        block = ctx.enter_context(nc.Block())

        def groups_until(t):
            return sum(-(-(u % TB + 1) // G) for u in range(t))

        def high_at(t):
            return range(0, 3) if t == 0 else range(t + 2, t + 3) if t + 2 < E else range(0)

        def low_at(t):
            return range(0, 2) if t == 0 else range(t + 1, t + 2) if t + 1 < E else range(0)

        def scales_at(t):
            return [g for g in range(LEAD // WG, E // WG) if WG * g + WG - 1 - LEAD == t]

        @block.sync
        def _(sp):
            for g in range(NG):
                sp.dma_start(xin[:, G * g:G * g + G, :], x_v[:, G * g:G * g + G, :]).then_inc(x_in[g], 16)

            def load_weights(n):
                if 2 * n >= RAW:
                    sp.wait_ge(wlo_done, 2 * n - RAW + 2)
                r = 2 * n % RAW
                sp.dma_start(raw[:, r:r + 2, 0, :], w1_v[:, 2 * n:2 * n + 2, :]).then_inc(w_in[n], 16)
                sp.dma_start(raw[:, r:r + 2, 1, :], w2_v[:, 2 * n:2 * n + 2, :]).then_inc(w_in[n], 16)

            load_weights(0)
            sp.wait_ge(blank_made, 1)
            sp.dma_start(slots_v, blank[:, None, :].broadcast_to([P, TILES, ROW])).then_inc(blank_sent, 16)
            for n in range(1, E // 2):
                load_weights(n)
                if n == 2:
                    sp.dma_start(wts_f[:, :, KIT_AT // 2 + B2F:KIT_AT // 2 + B2F + D],
                                 b2.rearrange("(a e) d -> a e d", a=1).broadcast_to([P, E, D])).then_inc(b2_in, 16)
            sp.wait_ge(rows_sent, 16 * K * NT)
            for n in range(NXG):
                a, z = XG * n, min(XG * n + XG, TILES)
                sp.dma_start(slots[:, a:z, :], slots_v[:, a:z, :]).then_inc(slots_in[n], 16)
            sp.wait_ge(expert_done, 1)
            sp.wait_ge(wlo_done, E)
            sp.wait_ge(b2_in, 16)
            for j in range(TILES):
                e = nc.s_assert_within(
                    sp.value_load(expert[0:1, j:j + 1]), 0, E - 1,
                    skip_runtime_bounds_check_because="a count of experts, held to E - 1 by a min")
                if j >= NST:
                    sp.wait_ge(y_done, j - NST + 1)
                sp.dma_start(stage_i[:, j % NST, :],
                             wts_i[:, bass.ds(e, 1), KIT_AT // 2:EW // 2].rearrange("p a c -> p (a c)")).then_inc(staged[j % NST], 16)
            for n in range(NYB):
                sp.wait_ge(y_sent[n], 16 * len(range(n, TILES, NYB)))
            for n in range(NYL):
                sp.dma_start(pairs[:, TYL * n:TYL * n + TYL, :, :],
                             pairs_v[:, TYL * n:TYL * n + TYL, :, :]).then_inc(pairs_in[n], 16)
            for n in range(NYL):
                sp.wait_ge(res_done, n + 1)
                sp.dma_start(out_v[:, TYL * n:TYL * n + TYL, :], xin[:, TYL * n:TYL * n + TYL, :]).then_inc(out_sent, 16)
            sp.wait_ge(out_sent, 16 * NYL)

        @block.gpsimd
        def _(pool):
            made = [0]

            def step(ins):
                made[0] += 1
                ins.then_inc(pool_step, 1)
                pool.wait_ge(pool_step, made[0])

            pool.memset(epsc[:, :], EPS)
            step(pool.memset(ident[:, :], 0.0))
            pool.affine_select(out=ident[:, :], in_=ident[:, :], compare_op=ALU.not_equal, fill=1.0,
                               base=0, pattern=[[-1, P]], channel_multiplier=1).then_inc(ident_made, 1)
            step(pool.memset(blank[:, :], 0.0))
            pool.iota(blank[:, :].bitcast(I32)[:, D:D + 1], pattern=[[0, 1]], base=1 << 20,
                      channel_multiplier=0).then_inc(blank_made, 1)
            pool.memset(before[:, :], 1.0)
            for e in range(E):
                pool.memset(rev[:, e, :], float(E - e))
            pool.memset(keep[:, :, 1:NT], 1.0)
            pool.memset(keep[:, :, 0:1], 0.0)
            pool.memset(ones16[:, :], 1.0)
            step(pool.memset(ones[:, :], 1.0))
            pool.affine_select(out=before[:, :], in_=before[:, :], compare_op=ALU.is_gt, fill=0.0,
                               base=0, pattern=[[1, P]], channel_multiplier=-1)
            for k in range(K):
                pool.iota(rows_i[:, k, :, D:D + 2], pattern=[[K * P, NT], [0, 2]], base=k, channel_multiplier=K)
            pool.memset(causal[:, :], 0.0)
            step(pool.iota(scratch_i[:, :], pattern=[[1, TILES + 1]], base=0, channel_multiplier=0))
            pool.tensor_copy(tileno[:, :], scratch_i[:, :])
            pool.affine_select(out=causal[:, :], in_=causal[:, :], compare_op=ALU.is_ge, fill=-HUGE,
                               base=0, pattern=[[-1, P]], channel_multiplier=1)
            pool.tensor_copy(ident16[:, :], ident[:, :]).then_inc(consts, 1)
            pool.memset(b1parts[:, :], 0.0)
            sel = wts[:, :, KIT_AT + SEL:KIT_AT + SEL + P]
            step(pool.memset(sel, 0.0))
            for half in range(2):
                step(pool.affine_select(out=sel, in_=sel, compare_op=ALU.not_equal, fill=1.0,
                                        base=-32 * half, pattern=[[-1, E], [0, P]], channel_multiplier=1))
            pool.wait_ge(bias_in, 16 * 11)
            for g in range(NG):
                pool.wait_ge(xn_done, g + 1)
                for t in range(G * g, G * g + G):
                    pool.tensor_tensor(xin[:, t, :], xin[:, t, :], bvb[:, :], ALU.add).then_inc(xbv_done, 1)
            pool.wait_ge(blank_sent, 16)
            pool.wait_ge(rows_done, NG)
            pool.wait_ge(slotrow_done, 1)
            for t in range(NT):
                for k in range(K):
                    pool.indirect_dma_start(slots_dram, bass.IndirectOffsetOnAxis(ap=slotrow[:, k, t:t + 1], axis=0),
                                            rows[:, k, t, :], None).then_inc(rows_sent, 16)
            for n in range(NXG):
                pool.wait_ge(slots_in[n], 16)
            for j in range(TILES):
                pool.wait_ge(y_done, j + 1)
                pool.indirect_dma_start(pairs_dram, bass.IndirectOffsetOnAxis(ap=slots_i[:, j, D:D + 1], axis=0),
                                        ybuf[:, j % NYB, :], None, bounds_check=NT * P * K - 1,
                                        oob_is_err=False).then_inc(y_sent[j % NYB], 16)

        @block.scalar
        def _(act):
            act.dma_start(wr[:, :], Wr).then_inc(bias_in, 16)
            act.dma_start(brb[:, :], br.rearrange("(a e) -> a e", a=1).broadcast_to([P, E])).then_inc(bias_in, 16)
            act.dma_start(bqk[:, 0:1], bq.rearrange("(p a) -> p a", a=1)).then_inc(bias_in, 16)
            act.dma_start(bqk[:, 1:2], bk.rearrange("(p a) -> p a", a=1)).then_inc(bias_in, 16)
            act.dma_start(bvb[:, :], bv.rearrange("(a d) -> a d", a=1).broadcast_to([P, D])).then_inc(bias_in, 16)
            act.dma_start(b1rows[0:E, :], b1).then_inc(bias_in, 16)
            act.dma_start(b1rows[32:32 + E, :], b1).then_inc(bias_in, 16)
            act.dma_start(b1cols[:, :, :], b1.rearrange("e (p c) -> p e c", p=P)).then_inc(bias_in, 16)
            for n, w in enumerate((Wq, Wk, Wv)):
                act.dma_start(wqkv[:, n, :], w).then_inc(bias_in, 16)

            act.wait_ge(ident_made, 1)

            def std_of(g):
                act.wait_ge(var_done, g + 1)
                nc.scalar.activation(std[:, G * g:G * g + G], mv[:, G * g:G * g + G, 1], ACT.Sqrt,
                                     bias=epsc[:, :]).then_inc(std_done, 1)

            def xT_copy(g):
                act.wait_ge(xT_done, g + 1)
                nc.scalar.copy(xT[:, G * P * g:G * P * (g + 1)], pT[g % 2][:, :]).then_inc(xT_copied, 1)

            def rows_hi(g):
                act.wait_ge(xn_done, g + 1)
                nc.scalar.copy(rows[:, 0, G * g:G * g + G, 0:D], xn[:, G * g:G * g + G, :]).then_inc(hi_rows, 1)

            for g in range(NG):
                std_of(g)
                if g:
                    xT_copy(g - 1)
                    rows_hi(g - 1)
            xT_copy(NG - 1)
            rows_hi(NG - 1)

            def squares(e):
                act.wait_ge(w_in[e // 2], 32)
                nc.scalar.activation(low_part(e), raw[:, e % RAW, :, :], ACT.Square, scale=16.0,
                                     accum_out=sumsq[:, e:e + 1]).then_inc(sq_done, 1)

            act.wait_ge(wT_done, 1)
            nc.scalar.copy(wqkvT[:, :, :], pO[1][:, 0:3 * D].rearrange("p (n d) -> p n d", n=3)).then_inc(wT_copied, 1)
            act.wait_ge(bias_in, 16 * 11)
            for g in range(NG):
                for n, to in enumerate((qT, kT)):
                    act.wait_ge(proj_done, 3 * g + n + 1)
                    nc.scalar.activation(to[:, G * P * g:G * P * (g + 1)], pA(3 * g + n), ACT.Identity,
                                         bias=bqk[:, n:n + 1]).then_inc(proj_copied, 1)
                act.wait_ge(proj_done, 3 * g + 3)
                nc.scalar.copy(v[:, G * g:G * g + G, :],
                               pA(3 * g + 2).rearrange("p (t d) -> p t d", t=G)).then_inc(proj_copied, 1)
                if g < NG - 1:
                    for e in range(2 * g, min(2 * g + 2, LEAD)):
                        squares(e)

            act.wait_ge(gap_done, 1)
            nc.scalar.activation(ex[:, :, :], ex[:, :, :], ACT.Exp)
            nc.scalar.activation(gap[:, :], gap[:, :], ACT.Exp).then_inc(ex_done, 1)

            def high(e):
                act.wait_ge(scale_done, e // WG + 1)
                nc.scalar.activation(high_part(e), raw[:, e % RAW, :, :], ACT.Copy,
                                     scale=wscale[:, e:e + 1]).then_inc(whi_done, 1)

            def softmax(t):
                n = (t % TB + 1) * P
                act.wait_ge(max_done, t + 1)
                if t >= 2:
                    act.wait_ge(pt_done, groups_until(t - 1))
                nc.scalar.activation(probs[:, t % 2, 0:n], pS[t % 2][:, 0:n], ACT.Exp, bias=negm[:, t:t + 1],
                                     scale=SCALE, accum_out=rsum[:, t:t + 1]).then_inc(exp_done, 1)

            def probsT_copy(t):
                u = groups_until(t)
                n = min(t % TB + 1, G) * P
                act.wait_ge(pt_done, u + 1)
                if t >= 1:
                    act.wait_ge(o_done, t)
                nc.scalar.copy(probsT[:, 0, 0:n], pT[0][:, 0:n]).then_inc(pt_act, 1)

            for t in range(NT):
                softmax(t)
                if t + LEAD < E:
                    squares(t + LEAD)
                probsT_copy(t)
                for e in high_at(t):
                    high(e)

            def xs_copy(j):
                act.wait_ge(xs_done, j + 1)
                if j >= 3:
                    act.wait_ge(l1_done, j - 2)
                nc.scalar.copy(xslot[:, j % 3, :], pT[j % 2][:, :].bitcast(F16)[:, 0:2 * D]).then_inc(xs_copied, 1)

            xs_copy(0)
            xs_copy(1)
            for j in range(TILES):
                act.wait_ge(l1_done, j + 1)
                if j >= NHB:
                    act.wait_ge(l2_done, j - NHB + 1)
                nc.scalar.activation(hid[:, j % NHB, 0, :], pA(j), ACT.Relu).then_inc(hi_done, 1)
                if j + 2 < TILES:
                    xs_copy(j + 2)

        @block.vector
        def _(dve):
            made = [0]

            def step(ins):
                made[0] += 1
                ins.then_inc(dve_step, 1)
                dve.wait_ge(dve_step, made[0])

            def moments(g):
                dve.wait_ge(x_in[g], 16)
                for t in range(G * g, G * g + G):
                    ins = dve.bn_stats(stats[:, t, :], xin[:, t, :])
                step(ins)
                for t in range(G * g, G * g + G):
                    ins = dve.bn_aggr(mv[:, t, :], stats[:, t, :])
                ins.then_inc(var_done, 1)

            def normalise(g):
                dve.wait_ge(std_done, g + 1)
                step(dve.reciprocal(rstd[:, G * g:G * g + G], std[:, G * g:G * g + G]))
                for t in range(G * g, G * g + G):
                    ins = dve.tensor_scalar(xn[:, t, :], xin[:, t, :], mv[:, t, 0:1], rstd[:, t:t + 1],
                                            ALU.subtract, ALU.mult)
                ins.then_inc(xn_done, 1)

            def rows_lo(g):
                dve.wait_ge(hi_rows, g + 1)
                step(dve.tensor_tensor(rows[:, 0, G * g:G * g + G, D:2 * D], xn[:, G * g:G * g + G, :],
                                       rows[:, 0, G * g:G * g + G, 0:D], ALU.subtract))
                dve.tensor_copy(rows[:, 1, G * g:G * g + G, 0:2 * D],
                                rows[:, 0, G * g:G * g + G, 0:2 * D]).then_inc(rows_done, 1)

            moments(0)
            for g in range(NG):
                if g + 1 < NG:
                    moments(g + 1)
                normalise(g)
                if g:
                    rows_lo(g - 1)
            rows_lo(NG - 1)

            dve.wait_ge(bias_in, 16 * 11)
            dve.wait_ge(consts, 1)
            dve.wait_ge(logits_done, NG)

            def over_tiles(a):
                return a[:, :, None].broadcast_to([P, E, NT])

            def over_experts(a):
                return a[:, None, :].broadcast_to([P, E, NT])

            def by_token(a):
                return a.rearrange("p e t -> p t e")

            step(dve.tensor_tensor(lg[:, :, :], pO[0][:, 0:NT * E].rearrange("p (t e) -> p e t", e=E),
                                   over_tiles(brb[:, :]), ALU.add))
            step(dve.tensor_reduce(best[:, 0, :], by_token(lg[:, :, :]), AX.X, ALU.max))
            for k, logits in enumerate((lg, lg2)):
                step(dve.tensor_tensor(hit[:, :, :], logits[:, :, :], over_experts(best[:, k, :]), ALU.is_equal))
                step(dve.tensor_tensor(hit[:, :, :], hit[:, :, :], rev[:, :, :], ALU.mult))
                step(dve.tensor_reduce(pick[:, :], by_token(hit[:, :, :]), AX.X, ALU.max))
                step(dve.tensor_tensor(oh[:, k, :, :], rev[:, :, :], over_experts(pick[:, :]), ALU.is_equal))
                if k == 0:
                    step(dve.scalar_tensor_tensor(out=lg2[:, :, :], in0=oh[:, 0, :, :], scalar=-HUGE,
                                                  in1=lg[:, :, :], op0=ALU.mult, op1=ALU.add))
                    step(dve.tensor_reduce(best[:, 1, :], by_token(lg2[:, :, :]), AX.X, ALU.max))
            dve.tensor_tensor(chosen[:, :, :], oh[:, 0, :, :], oh[:, 1, :, :], ALU.add).then_inc(chosen_done, 1)
            dve.tensor_tensor(ex[:, :, :], lg[:, :, :], over_experts(best[:, 0, :]), ALU.subtract)
            dve.tensor_tensor(gap[:, :], best[:, 1, :], best[:, 0, :], ALU.subtract).then_inc(gap_done, 1)

            dve.wait_ge(ranks_done, 1)
            rank = pO[0][:, 0:E * NT]
            total = pO[0][:, E * NT:2 * E * NT]

            def flat(a):
                return a.rearrange("p e t -> p (e t)")

            step(dve.tensor_tensor_scan(flat(incl[:, :, :]), flat(keep[:, :, :]), total, 0.0, ALU.mult, ALU.add))
            step(dve.tensor_tensor(flat(pos[:, :, :]), flat(incl[:, :, :]), total, ALU.subtract))
            step(dve.tensor_tensor(flat(pos[:, :, :]), flat(pos[:, :, :]), rank, ALU.add))
            step(dve.tensor_scalar(cnt[:, :], incl[:, :, NT - 1], float(P - 1), None, ALU.add))
            step(dve.tensor_scalar(ntile[:, :], cnt[:, :], P.bit_length() - 1, None, ALU.logical_shift_right))
            step(dve.tensor_copy(ntilef[:, :], ntile[:, :]))
            step(dve.tensor_tensor_scan(cum[:, :], ones[:, 0:E], ntilef[:, :], 0.0, ALU.mult, ALU.add))
            step(dve.tensor_tensor(start[:, :], cum[:, :], ntilef[:, :], ALU.subtract))
            step(dve.scalar_tensor_tensor(out=pos[:, :, :], in0=over_tiles(start[:, :]), scalar=float(P),
                                          in1=pos[:, :, :], op0=ALU.mult, op1=ALU.add))
            for k in range(K):
                step(dve.tensor_tensor(hit[:, :, :], oh[:, k, :, :], pos[:, :, :], ALU.mult))
                step(dve.tensor_reduce(posk[:, k, :], by_token(hit[:, :, :]), AX.X, ALU.add))
            step(dve.tensor_copy(posi[:, :, :], posk[:, :, :]))
            dve.tensor_scalar(posr[:, :, :], posi[:, :, :], P.bit_length() - 1, None, ALU.logical_shift_right)
            step(dve.tensor_scalar(posi[:, :, :], posi[:, :, :], P - 1, None, ALU.bitwise_and))
            dve.scalar_tensor_tensor(out=slotrow[:, :, :], in0=posi[:, :, :], scalar=float(TILES),
                                     in1=posr[:, :, :], op0=ALU.mult, op1=ALU.add).then_inc(slotrow_done, 1)
            step(dve.tensor_tensor(past[:, :, :], cum[0:1, None, :].broadcast_to([1, TILES + 1, E]),
                                   tileno[0:1, :, None].broadcast_to([1, TILES + 1, E]), ALU.is_le))
            step(dve.tensor_reduce(expertf[:, :], past[:, :, :], AX.X, ALU.add))
            dve.tensor_scalar(expert[:, :], expertf[:, :], float(E - 1), None, ALU.min).then_inc(expert_done, 1)

            dve.wait_ge(ex_done, 1)
            step(dve.tensor_reduce(exsum[:, :], by_token(ex[:, :, :]), AX.X, ALU.add))
            step(dve.reciprocal(gate[:, 0, :], exsum[:, :]))
            dve.tensor_tensor(gate[:, 1, :], gate[:, 0, :], gap[:, :], ALU.mult)
            def b1_norms():
                step(dve.tensor_tensor(b1sq[:, :, :], b1cols[:, :, :], b1cols[:, :, :], ALU.mult))
                dve.tensor_reduce(b1sum[:, :], b1sq[:, :, :], AX.X, ALU.add).then_inc(b1sum_done, 1)

            def scales(g):
                s = slice(WG * g, WG * g + WG)
                dve.wait_ge(sums_done, g + 1)
                step(dve.tensor_scalar(nrm[:, s], pO[1][:, 0:WG], 2.0 ** -120, None, ALU.max))
                step(dve.tensor_scalar(expo[:, s], nrm[:, s].bitcast(I32), 23, None, ALU.logical_shift_right))
                step(dve.tensor_scalar(expo2[:, s], expo[:, s], 127.0, None, ALU.add))
                step(dve.tensor_scalar(pw[:, s], expo2[:, s], 1, 23, ALU.logical_shift_right,
                                       ALU.logical_shift_left))
                step(dve.reciprocal(inv[:, s], pw[:, s].bitcast(F32)))
                dve.tensor_scalar(wscale[:, s], inv[:, s], 2.0 ** 13, None, ALU.mult).then_inc(scale_done, 1)
                dve.scalar_tensor_tensor(out=wts_f[:, s, KIT_AT // 2 + CF], in0=pw[:, s].bitcast(F32),
                                         scalar=2.0 ** -26, in1=pw[:, s].bitcast(F32),
                                         op0=ALU.mult, op1=ALU.mult)

            def low(e):
                dve.wait_ge(whi_done, e + 1)
                dve.wait_ge(scale_done, e // WG + 1)
                dve.scalar_tensor_tensor(out=low_part(e), in0=raw[:, e % RAW, :, :], scalar=wscale[:, e:e + 1],
                                         in1=high_part(e), op0=ALU.mult, op1=ALU.subtract).then_inc(wlo_done, 1)

            def row_max(t):
                i = t % TB
                sc = pS[t % 2]
                dve.wait_ge(s_done, t + 1)
                if i:
                    step(dve.tensor_reduce(m0[:, t:t + 1], sc[:, 0:i * P], AX.X, ALU.max))
                step(dve.tensor_tensor_reduce(out=sc[:, i * P:(i + 1) * P], in0=sc[:, i * P:(i + 1) * P],
                                              in1=causal[:, :], scale=1.0, scalar=m0[:, t:t + 1] if i else -HUGE,
                                              op0=ALU.add, op1=ALU.max, accum_out=m1[:, t:t + 1]))
                dve.tensor_scalar(negm[:, t:t + 1], m1[:, t:t + 1], -SCALE, None, ALU.mult).then_inc(max_done, 1)

            def probsT_copy(t):
                if t % TB + 1 > G:
                    n = (t % TB + 1 - G) * P
                    dve.wait_ge(pt_done, groups_until(t) + 2)
                    if t >= 1:
                        dve.wait_ge(o_done, t)
                    dve.tensor_copy(probsT[:, 1, 0:n], pT[1][:, 0:n]).then_inc(pt_dve, 1)

            def attended(t):
                dve.wait_ge(exp_done, t + 1)
                step(dve.reciprocal(rinv[:, t:t + 1], rsum[:, t:t + 1]))
                dve.wait_ge(o_done, t + 1)
                dve.wait_ge(xbv_done, t + 1)
                dve.scalar_tensor_tensor(out=xin[:, t, :], in0=pO[0][:, 0:D], scalar=rinv[:, t:t + 1],
                                         in1=xin[:, t, :], op0=ALU.mult, op1=ALU.add).then_inc(o_read, 1)

            b1_norms()
            for g in range(LEAD // WG):
                scales(g)
            row_max(0)
            for t in range(NT):
                if t + 1 < NT:
                    row_max(t + 1)
                probsT_copy(t)
                attended(t)
                for g in scales_at(t):
                    scales(g)
                for e in low_at(t):
                    low(e)
            hi_b, lo_b = b1parts[0:E, :], b1parts[32:32 + E, :]
            for at in (0, 32):
                dve.tensor_tensor(b1tmp[at:at + E, :], wscale[at:at + E, :], ident[at:at + E, at:at + E], ALU.mult)
            step(dve.memset(b1s[:, :], 0.0))
            for at in (0, 32):
                ins = dve.tensor_reduce(b1s[at:at + E, :], b1tmp[at:at + E, :], AX.X, ALU.add)
            step(ins)
            for at in (0, 32):
                ins = dve.tensor_scalar(b1rows[at:at + E, :], b1rows[at:at + E, :], b1s[at:at + E, :], None, ALU.mult)
            step(ins)
            step(dve.tensor_copy(hi_b, b1rows[0:E, :]))
            step(dve.tensor_copy(lo_b, b1rows[32:32 + E, :]))
            step(dve.tensor_tensor(b1rows[32:32 + E, :], b1rows[32:32 + E, :], lo_b, ALU.subtract))
            dve.tensor_copy(lo_b, b1rows[32:32 + E, :]).then_inc(b1_done, 1)

            def y_of(j):
                dve.wait_ge(l2_done, j + 1)
                dve.wait_ge(staged[j % NST], 16 * (j // NST + 1))
                if j >= NYB:
                    dve.wait_ge(y_sent[j % NYB], 16 * (j // NYB))
                dve.scalar_tensor_tensor(out=ybuf[:, j % NYB, :], in0=pO[j % 2][:, 0:D],
                                         scalar=stage_f[:, j % NST, CF:CF + 1],
                                         in1=stage_f[:, j % NST, B2F:B2F + D],
                                         op0=ALU.mult, op1=ALU.add).then_inc(y_done, 1)

            for j in range(TILES):
                dve.wait_ge(hi_done, j + 1)
                dve.scalar_tensor_tensor(out=hid[:, j % NHB, 1, :], in0=pA(j), scalar=0.0,
                                         in1=hid[:, j % NHB, 0, :], op0=ALU.max,
                                         op1=ALU.subtract).then_inc(lo_done, 1)
                if j >= 2:
                    y_of(j - 2)
            y_of(TILES - 2)
            y_of(TILES - 1)

            for n in range(NYL):
                dve.wait_ge(pairs_in[n], 16)
                for k in range(K):
                    for t in range(TYL * n, TYL * n + TYL):
                        ins = dve.scalar_tensor_tensor(out=xin[:, t, :], in0=pairs[:, t, k, :],
                                                       scalar=gate[:, k, t:t + 1], in1=xin[:, t, :],
                                                       op0=ALU.mult, op1=ALU.add)
                    if k == 0:
                        step(ins)
                ins.then_inc(res_done, 1)

        @block.tensor
        def _(pe):
            pe.wait_ge(ident_made, 1)

            def x_transposes(g):
                pe.wait_ge(xn_done, g + 1)
                if g >= 2:
                    pe.wait_ge(xT_copied, g - 1)
                for i in range(G):
                    ins = pe.transpose(pT[g % 2][:, i * P:(i + 1) * P], xn[:, G * g + i, :], ident[:, :])
                ins.then_inc(xT_done, 1)

            def router(g):
                pe.wait_ge(xT_copied, g + 1)
                for t in range(G * g, G * g + G):
                    ins = pe.matmul(pO[0][:, t * E:(t + 1) * E], xT[:, t * P:(t + 1) * P], wr[:, :],
                                    start=True, stop=True)
                ins.then_inc(logits_done, 1)

            for g in range(NG):
                x_transposes(g)
                if g == 1:
                    pe.wait_ge(bias_in, 16 * 11)
                if g:
                    router(g - 1)
            for n in range(3):
                ins = pe.transpose(pO[1][:, n * D:(n + 1) * D], wqkv[:, n, :], ident[:, :])
            ins.then_inc(wT_done, 1)
            router(NG - 1)

            pe.wait_ge(wT_copied, 1)
            for g in range(NG):
                cols = slice(G * P * g, G * P * (g + 1))
                for n in range(3):
                    if 3 * g + n >= 4:
                        pe.wait_ge(proj_copied, 3 * g + n - 3)
                    if n < 2:
                        ins = pe.matmul(pA(3 * g + n), wqkvT[:, n, :], xT[:, cols], start=True, stop=True)
                    else:
                        for i in range(G):
                            t = G * g + i
                            ins = pe.matmul(pA(3 * g + 2)[:, i * D:(i + 1) * D], xT[:, t * P:(t + 1) * P],
                                            wqkvT[:, 2, :], start=True, stop=True)
                    ins.then_inc(proj_done, 1)
                if g == 1:
                    pe.wait_ge(chosen_done, 1)
                    pe.wait_ge(consts, 1)
                    m = chosen[:, :, :].rearrange("p e t -> p (e t)")
                    pe.matmul(pO[0][:, 0:E * NT], before[:, :], m, start=True, stop=True)
                    pe.matmul(pO[0][:, E * NT:2 * E * NT], ones16[:, :], m, start=True,
                              stop=True).then_inc(ranks_done, 1)

            def scores(t):
                n = (t % TB + 1) * P
                if t >= 2:
                    pe.wait_ge(exp_done, t - 1)
                if t == 0:
                    pe.wait_ge(proj_copied, 3 * NG)
                at = t // TB * S
                for a in range(0, n, 512):
                    z = min(a + 512, n)
                    ins = pe.matmul(pS[t % 2][:, a:z], qT[:, t * P:(t + 1) * P], kT[:, at + a:at + z],
                                    start=True, stop=True)
                ins.then_inc(s_done, 1)

            def probs_transposes(t):
                pe.wait_ge(exp_done, t + 1)
                if t >= 1:
                    pe.wait_ge(pt_act, t)
                    second = sum(u % TB + 1 > G for u in range(t))
                    if second:
                        pe.wait_ge(pt_dve, second)
                for a in range(0, t % TB + 1, G):
                    for j in range(a, min(a + G, t % TB + 1)):
                        ins = pe.transpose(pT[a // G][:, (j - a) * P:(j - a + 1) * P],
                                           probs[:, t % 2, j * P:(j + 1) * P], ident[:, :])
                    ins.then_inc(pt_done, 1)

            def attend(t):
                i = t % TB
                pe.wait_ge(pt_act, t + 1)
                if i + 1 > G:
                    pe.wait_ge(pt_dve, sum(u % TB + 1 > G for u in range(t + 1)))
                if t:
                    pe.wait_ge(o_read, t)
                else:
                    pe.wait_ge(slotrow_done, 1)
                for j in range(i + 1):
                    ins = pe.matmul(pO[0][:, 0:D], probsT[:, j // G, j % G * P:(j % G + 1) * P],
                                    v[:, t // TB * TB + j, :], start=(j == 0), stop=(j == i))
                ins.then_inc(o_done, 1)

            def weight_sums(g):
                pe.wait_ge(sq_done, WG * (g + 1))
                pe.wait_ge(b1sum_done, 1)
                if g:
                    pe.wait_ge(scale_done, g)
                s = slice(WG * g, WG * g + WG)
                pe.matmul(pO[1][:, 0:WG], ones[:, :], sumsq[:, s], start=True, stop=False)
                pe.matmul(pO[1][:, 0:WG], ones[:, :], b1sum[:, s], start=False, stop=True).then_inc(sums_done, 1)

            for g in range(LEAD // WG):
                weight_sums(g)
            scores(0)
            scores(1)
            for t in range(NT):
                probs_transposes(t)
                if t + 2 < NT:
                    scores(t + 2)
                attend(t)
                for g in scales_at(t):
                    weight_sums(g)

            def slot_transposes(j):
                pe.wait_ge(slots_in[j // XG], 16)
                if j >= 2:
                    pe.wait_ge(xs_copied, j - 1)
                else:
                    pe.wait_ge(pt_act, NT)
                to = pT[j % 2][:, :].bitcast(F16)
                pe.transpose(to[:, 0:D], slots[:, j, 0:D], ident16[:, :])
                pe.transpose(to[:, D:2 * D], slots[:, j, D:2 * D], ident16[:, :]).then_inc(xs_done, 1)

            def expert_of(j):
                return nc.s_assert_within(
                    pe.value_load(expert[0:1, j:j + 1]), 0, E - 1,
                    skip_runtime_bounds_check_because="a count of experts, held to E - 1 by a min")

            def result(r, c):
                s = stage[:, r % NST, :]
                y = pO[r % 2][:, 0:D]
                h_hi, h_lo = hid[:, r % NHB, 0, c * P:(c + 1) * P], hid[:, r % NHB, 1, c * P:(c + 1) * P]
                w_hi, w_lo = s[:, W2_HI + c * P:W2_HI + (c + 1) * P], s[:, W2_LO + c * P:W2_LO + (c + 1) * P]
                pe.matmul(y, h_hi, w_hi, start=(c == 0), stop=False)
                pe.matmul(y, h_hi, w_lo, start=False, stop=False)
                return pe.matmul(y, h_lo, w_hi, start=False, stop=(c == NCH - 1))

            def result_waits(r):
                pe.wait_ge(lo_done, r + 1)
                if r >= 2:
                    pe.wait_ge(y_done, r - 1)

            def hidden(j, e, r):
                pe.wait_ge(xs_copied, j + 1)
                pe.wait_ge(staged[j % NST], 16 * (j // NST + 1))
                if j >= 4:
                    pe.wait_ge(lo_done, j - 3)
                bank = pA(j)
                x_hi, x_lo = xslot[:, j % 3, 0:D], xslot[:, j % 3, D:2 * D]
                for c in range(NCH):
                    pe.matmul(bank[:, c * P:(c + 1) * P], b1parts[:, c:HID:NCH],
                              stage[:, j % NST, SEL:SEL + P], start=(c == 0), stop=False, skip_group_check=True)
                after = None
                for c in range(NCH):
                    to = bank[:, c * P:(c + 1) * P]
                    w_hi = wts[:, bass.ds(e, 1), W1_HI + c:W1_HI + HID:NCH].rearrange("p a h -> p (a h)")
                    pe.matmul(to, w_hi, x_hi, start=False, stop=False, skip_group_check=True)
                    pe.matmul(to, w_hi, x_lo, start=False, stop=False, skip_group_check=True)
                    w_lo = wts[:, bass.ds(e, 1), W1_LO + c:W1_LO + HID:NCH].rearrange("p a h -> p (a h)")
                    ins = pe.matmul(to, w_lo, x_hi, start=False, stop=(c == NCH - 1), skip_group_check=True)
                    if c == 1 and j + 1 < TILES:
                        after = expert_of(j + 1)
                    if r is not None:
                        if c == 1:
                            result_waits(r)
                            result(r, 0)
                            result(r, 1)
                        elif c > 1:
                            last = result(r, c)
                ins.then_inc(l1_done, 1)
                if r is not None:
                    last.then_inc(l2_done, 1)
                return after

            slot_transposes(0)
            slot_transposes(1)
            pe.wait_ge(expert_done, 1)
            pe.wait_ge(wlo_done, E)
            pe.wait_ge(b1_done, 1)
            pe.wait_ge(o_read, NT)
            e = expert_of(0)
            for j in range(TILES):
                e = hidden(j, e, j - 2 if j >= 2 else None)
                if j + 2 < TILES:
                    slot_transposes(j + 2)
            for r in (TILES - 2, TILES - 1):
                result_waits(r)
                for c in range(NCH):
                    last = result(r, c)
                last.then_inc(l2_done, 1)


_INS = ["L0_attn_x", "L0_attn_Wk", "L0_attn_bk", "L0_attn_Wq", "L0_attn_bq", "L0_attn_Wv", "L0_attn_bv",
        "L0_ffn_Wr", "L0_ffn_br", "L0_ffn_W1", "L0_ffn_b1", "L0_ffn_W2", "L0_ffn_b2"]


def kernel(**inputs):
    import numpy as np
    import concourse.bacc as bacc
    from concourse import mybir as mb
    from concourse.bass_utils import run_bass_kernel_spmd

    nc = bacc.Bacc("TRN2", target_bir_lowering=False, num_devices=1)
    arrays, args = {}, []
    for name in _INS:
        a = np.ascontiguousarray(inputs[name])
        arrays[f"in_{name}"] = a
        args.append(nc.dram_tensor(f"in_{name}", a.shape, mb.dt.from_np(a.dtype), kind="ExternalInput").ap())
    out = nc.dram_tensor("out_0", inputs["L0_attn_x"].shape, F32, kind="ExternalOutput").ap()
    attention_and_top2_experts(nc, *args, out)
    r = run_bass_kernel_spmd(nc, [arrays], core_ids=[0])
    return r.results[0]["out_0"]
```

```python
from contextlib import ExitStack

import concourse.bass as bass
from concourse import mybir

ALU = mybir.AluOpType
ACT = mybir.ActivationFunctionType
AX = mybir.AxisListType
F32 = mybir.dt.float32
F16 = mybir.dt.float16
BF16 = mybir.dt.bfloat16
I32 = mybir.dt.int32

P = 128
HUGE = 3.0e38


def attention_and_top2_experts(nc, x, Wk, bk, Wq, bq, Wv, bv, Wr, br, W1, b1, W2, b2, out):
    B, S, D = x.shape
    E = Wr.shape[1]
    HID = W1.shape[2]
    K = 2
    NT = B * S // P
    TB = S // P
    NCH = HID // P
    TILES = K * NT + E - 1
    EPS = 1e-5
    SCALE = float(D) ** -0.5
    G = 4
    NG = NT // G
    assert D == P and HID == NCH * P

    ROW = 2 * D + 4
    W1_HI, W1_LO, KIT_AT = 0, HID, 2 * HID
    W2_HI, W2_LO, SEL, B2F = 0, HID, 2 * HID, (2 * HID + P) // 2
    CF = B2F + D
    KIT = 2 * (CF + 1)
    EW = KIT_AT + KIT
    RAW = 6
    WG = 2
    NST, NHB, NYB = 7, 3, 6
    XG = [0, 6, 16, 32, TILES]
    WL = [*range(0, E - 1, 2), E - 1, E]
    NYL = 8
    TYL = NT // NYL
    WARM_UP = 14
    LATE = 3

    slots_dram = nc.dram_tensor("slots_dram", (P * TILES, ROW // 2), I32).ap()
    pairs_dram = nc.dram_tensor("pairs_dram", (NT * P * K, D), F32).ap()

    with ExitStack() as ctx:
        def sb(name, shape, dt):
            return ctx.enter_context(nc.sbuf_tensor(name, shape, dt))

        def sem(name):
            return ctx.enter_context(nc.semaphore(name))

        xin = sb("xin", [P, NT, D], F32)
        xn = sb("xn", [P, NT, D], F32)
        xT = sb("xT", [P, NT * P], F32)
        qT = sb("qT", [P, NT * P], F32)
        kT = sb("kT", [P, NT * P], F32)
        v = sb("v", [P, NT, D], F32)
        wts = sb("wts", [P, E, EW], F16)
        raw = sb("raw", [P, RAW, 2, HID], F32)
        probsT0 = sb("probsT0", [P, 2, G * P], F32)
        wr = sb("wr", [P, E], F32)
        brb = sb("brb", [P, E], F32)
        bqk = sb("bqk", [P, 2], F32)
        b1rows = sb("b1rows", [P, HID], F32)
        b1parts = [sb(f"b1parts{n}", [P, HID], F16) for n in range(2)]
        mv = sb("mv", [P, NT, 2], F32)
        std = sb("std", [P, NT], F32)
        rstd = sb("rstd", [P, NT], F32)
        epsc = sb("epsc", [P, 1], F32)
        ident = sb("ident", [P, P], F32)
        ident16 = sb("ident16", [P, P], F16)
        causal = sb("causal", [P, S], BF16)
        ones = sb("ones", [P, P], F32)
        tileno = sb("tileno", [P, 1], F32)
        scratch_i = sb("scratch_i", [P, 1], I32)
        past = sb("past", [P, E], F32)
        best = sb("best", [P, K, NT], F32)
        pick = sb("pick", [P, NT], F32)
        gap = sb("gap", [P, NT], F32)
        slotrow = sb("slotrow", [P, K, NT], I32)
        cnt = sb("cnt", [P, E], I32)
        ntile = sb("ntile", [P, E], I32)
        ntilef = sb("ntilef", [P, E], F32)
        cum = sb("cum", [P, E], F32)
        start = sb("start", [P, E], F32)
        expertf = sb("expertf", [P, 1], F32)
        expert = sb("expert", [P, 1], I32)
        sumsq = sb("sumsq", [P, E], F32)
        b1sum = sb("b1sum", [P, E], F32)
        expo = sb("expo", [P, E], I32)
        expo2 = sb("expo2", [P, E], I32)
        pw = sb("pw", [P, E], I32)
        wscale = sb("wscale", [P, E], F32)
        b1s = sb("b1s", [P, 1], F32)
        b1tmp = sb("b1tmp", [P, E], F32)
        diag = sb("diag", [P, E], F32)
        negm = sb("negm", [P, NT], F32)
        rsum = sb("rsum", [P, NT], F32)
        rinv = sb("rinv", [P, NT], F32)

        slot_space = sb("slot_space", [P, TILES * ROW], F16)
        slots = slot_space[:, :].rearrange("p (t c) -> p t c", t=TILES)
        rows = slot_space[:, 0:K * NT * ROW].rearrange("p (k t c) -> p k t c", k=K, t=NT)

        stage_w, hid_w, xslot_w, ybuf_w = NST * KIT, NHB * 2 * HID, 3 * 2 * D, NYB * 2 * D
        space = sb("space", [P, stage_w + ybuf_w], F16)
        stage = space[:, 0:stage_w].rearrange("p (s c) -> p s c", s=NST)
        ybuf = space[:, stage_w:stage_w + ybuf_w].bitcast(F32).rearrange("p (s d) -> p s d", s=NYB)

        taken = [0]

        def early(n, parts=P):
            a = 2 * taken[0]
            taken[0] += n
            assert 2 * taken[0] <= stage_w + ybuf_w
            return space[0:parts, a:a + 2 * n].bitcast(F32)

        def per_expert(n=1):
            return early(n * E * NT).rearrange("p (e t) -> p e t", t=NT)

        def early_f16(n):
            return early(n // 2).bitcast(F16)

        bvb = early(D)
        stats = early(NT * 6).rearrange("p (t c) -> p t c", t=NT)
        later = early_f16(P)
        ones16 = early_f16(P)
        blank = early(ROW // 2).bitcast(I32)
        chosen = early_f16(E * NT).rearrange("p (e t) -> p e t", e=E)
        sofar = early_f16(E * NT).rearrange("p (e t) -> p e t", e=E)
        exsum = early(NT)
        posk = early(K * NT).rearrange("p (k t) -> p k t", k=K)
        posi = early(K * NT).bitcast(I32).rearrange("p (k t) -> p k t", k=K)
        posr = early(K * NT).bitcast(I32).rearrange("p (k t) -> p k t", k=K)
        wqkv = early(3 * D).rearrange("p (n d) -> p n d", n=3)
        wqkvT = early(3 * D).rearrange("p (n d) -> p n d", n=3)
        b1cols = early(E * NCH).rearrange("p (e c) -> p e c", e=E)
        b1sq = early(E * NCH).rearrange("p (e c) -> p e c", e=E)
        rev, keep = per_expert(), per_expert()
        lg, lg2, hit, ex, pos = (per_expert() for _ in range(5))
        oh = early(K * E * NT).rearrange("p (k e t) -> p k e t", k=K, e=E)

        hid = xT[:, 0:hid_w // 2].bitcast(F16).rearrange("p (s a h) -> p s a h", s=NHB, a=2)
        xslot = xT[:, hid_w // 2:(hid_w + xslot_w) // 2].bitcast(F16).rearrange("p (s c) -> p s c", s=3)

        probsT = [probsT0, xT[:, 0:2 * G * P].rearrange("p (a n) -> p a n", a=2)]
        probs = xn[:, :, :].rearrange("p t d -> p (t d)").rearrange("p (a n) -> p a n", a=2)
        pairs = raw[:, 0:4, :, :].rearrange("p r w h -> p (r w h)").rearrange(
            "p (t k d) -> p t k d", k=K, d=D)
        slots_f = slot_space[:, :].bitcast(F32).rearrange("p (t c) -> p t c", t=TILES)
        rows_f = slot_space[:, 0:K * NT * ROW].bitcast(F32).rearrange("p (k t c) -> p k t c", k=K, t=NT)
        slots_i = slot_space[:, :].bitcast(I32).rearrange(
            "p (t c) -> p t c", t=TILES)
        rows_i = slot_space[:, 0:K * NT * ROW].bitcast(I32).rearrange(
            "p (k t c) -> p k t c", k=K, t=NT)
        wts_f = wts[:, :, :].rearrange("p e c -> p (e c)").bitcast(F32).rearrange("p (e c) -> p e c", e=E)
        stage_f = space[:, 0:stage_w].bitcast(F32).rearrange(
            "p (s c) -> p s c", s=NST)

        wts_i = wts[:, :, :].rearrange("p e c -> p (e c)").bitcast(I32).rearrange("p (e c) -> p e c", e=E)
        stage_i = space[:, 0:stage_w].bitcast(I32).rearrange("p (s c) -> p s c", s=NST)

        pS = [ctx.enter_context(nc.psum_tensor(f"pS{n}", [P, 1024], F32)) for n in range(2)]
        pT = [ctx.enter_context(nc.psum_tensor(f"pT{n}", [P, 512], F32)) for n in range(2)]
        pO = [ctx.enter_context(nc.psum_tensor(f"pO{n}", [P, 512], F32)) for n in range(2)]

        def pA(n):
            return pS[n % 4 // 2][:, 512 * (n % 2):512 * (n % 2) + 512]

        x_in = [sem(f"x_in{g}") for g in range(NG)]
        router_in = sem("router_in")
        proj_in = sem("proj_in")
        b1cols_in = sem("b1cols_in")
        bias_in = sem("bias_in")
        b2_in = sem("b2_in")
        w_in = [sem(f"w_in{n}") for n in range(len(WL) - 1)]
        blank_sent = sem("blank_sent")
        rows_sent = sem("rows_sent")
        slots_in = [sem(f"slots_in{n}") for n in range(len(XG) - 1)]
        staged = [sem(f"staged{n}") for n in range(NST)]
        y_sent = [sem(f"y_sent{n}") for n in range(NYB)]
        pairs_in = [sem(f"pairs_in{n}") for n in range(NYL)]
        out_sent = sem("out_sent")
        ident_made = sem("ident_made")
        blank_made = sem("blank_made")
        consts = sem("consts")
        pool_step = sem("pool_step")
        dve_step = sem("dve_step")
        wT_done = sem("wT_done")
        wT_copied = sem("wT_copied")
        var_done = sem("var_done")
        std_done = sem("std_done")
        xn_done = sem("xn_done")
        xT_done = sem("xT_done")
        xT_copied = sem("xT_copied")
        hi_rows = sem("hi_rows")
        lo_rows = sem("lo_rows")
        rows_done = sem("rows_done")
        logits_done = sem("logits_done")
        chosen_done = sem("chosen_done")
        ranks_done = sem("ranks_done")
        slotrow_done = sem("slotrow_done")
        expert_done = sem("expert_done")
        gap_done = sem("gap_done")
        ex_done = sem("ex_done")
        proj_done = sem("proj_done")
        proj_copied = sem("proj_copied")
        xbv_done = sem("xbv_done")
        sq_done = sem("sq_done")
        b1sum_done = sem("b1sum_done")
        sums_done = sem("sums_done")
        scale_done = sem("scale_done")
        whi_act = sem("whi_act")
        whi_pool = sem("whi_pool")
        wlo_done = sem("wlo_done")
        b1s_done = sem("b1s_done")
        b1hi_done = sem("b1hi_done")
        b1_done = sem("b1_done")
        s_done = sem("s_done")
        max_done = sem("max_done")
        exp_done = sem("exp_done")
        pt_done = sem("pt_done")
        pt_act = sem("pt_act")
        pt_dve = sem("pt_dve")
        rinv_done = sem("rinv_done")
        o_done = sem("o_done")
        o_read = sem("o_read")
        xs_done = sem("xs_done")
        xs_copied = sem("xs_copied")
        l1_done = sem("l1_done")
        hi_done = sem("hi_done")
        lo_done = sem("lo_done")
        l2_done = sem("l2_done")
        y_done = sem("y_done")
        y_gated = sem("y_gated")
        res_done = sem("res_done")
        res_pool = sem("res_pool")

        x_v = x.rearrange("b (t p) d -> p (b t) d", p=P)
        out_v = out.rearrange("b (t p) d -> p (b t) d", p=P)
        slots_v = slots_dram.rearrange("(p t) c -> p t c", p=P)
        pairs_v = pairs_dram.rearrange("(t p k) d -> p t k d", p=P, k=K)
        w1_v = W1.rearrange("e d h -> d e h")
        w2_v = W2.rearrange("e (p c) m -> p e (c m)", p=P)

        def high_part(e):
            return wts[:, e, 0:4 * HID].rearrange("p (w a h) -> p w a h", w=2, a=2)[:, :, 0, :]

        def low_part(e):
            return wts[:, e, 0:4 * HID].rearrange("p (w a h) -> p w a h", w=2, a=2)[:, :, 1, :]

        block = ctx.enter_context(nc.Block())

        def groups_until(t):
            return sum(-(-(u % TB + 1) // G) for u in range(t))

        SQUARES = {3: (6,), 4: (7,), 5: (8,), 6: (9,), 8: (10,), 9: (11,), 11: (12,)}
        SCALES = {1: (0, 1, 2), 6: (3,), 8: (4,), 11: (5,)}
        HIGH = {0: (2,), 1: (3,), 2: (4,), 3: (5,), 5: (6,), 6: (7,), 7: (8,), 10: (9,)}
        LOW = {0: (0,), 1: (1,), 2: (2,), 3: (3,), 4: (4,), 5: (5,), 6: (6,), 7: (7,), 10: (8,), 11: (9,)}
        B1_AT = 10
        POOL_HIGH = (0, 1, 10, 11, 13, 15)
        SQUARES_LATE = {-1: (13,), 1: (14,), 2: (15,)}
        SCALES_LATE, GROUPS_LATE = 4, (6, 7)
        HIGH_LATE = {5: (12,), 7: (14,)}
        POOL_HIGH_LATE = {2: 4, 4: 5}
        LOW_LATE = {1: (11,), 6: (12,), 7: (13,), 8: (14,), 10: (15,)}
        B1_HIGH_LATE, B1_LOW_LATE, B1_SECOND = 6, 9, WG * GROUPS_LATE[0]

        POOL_SUMS = (1, 4, 6)
        SUMS = [n for n in range(NYL) if n not in POOL_SUMS]

        def sums_bank(g):
            if g in GROUPS_LATE:
                return pT[SCALES_LATE % 2]
            return pO[[t for t in SCALES if g in SCALES[t]][0] % 2]

        @block.sync
        def _(sp):
            def load_x(g):
                sp.dma_start(xin[:, G * g:G * g + G, :], x_v[:, G * g:G * g + G, :]).then_inc(x_in[g], 16)

            load_x(0)
            load_x(1)
            sp.dma_start(wr[:, :], Wr).then_inc(router_in, 16)
            load_x(2)
            sp.dma_start(brb[:, :], br.rearrange("(a e) -> a e", a=1).broadcast_to([P, E])).then_inc(router_in, 16)
            load_x(3)
            for n, w in enumerate((Wq, Wk, Wv)):
                sp.dma_start(wqkv[:, n, :], w).then_inc(proj_in, 16)
            sp.dma_start(bqk[:, 0:1], bq.rearrange("(p a) -> p a", a=1)).then_inc(proj_in, 16)
            sp.dma_start(bqk[:, 1:2], bk.rearrange("(p a) -> p a", a=1)).then_inc(proj_in, 16)

            def load_weights(n):
                a, z = WL[n], WL[n + 1]
                if z > RAW:
                    sp.wait_ge(wlo_done, z - RAW)
                here = slice(a % RAW, a % RAW + z - a)
                sp.dma_start(raw[:, here, 0, :], w1_v[:, a:z, :]).then_inc(w_in[n], 16)
                sp.dma_start(raw[:, here, 1, :], w2_v[:, a:z, :]).then_inc(w_in[n], 16)

            load_weights(0)
            sp.dma_start(b1cols[:, :, :], b1.rearrange("e (p c) -> p e c", p=P)).then_inc(b1cols_in, 16)
            load_weights(1)
            load_weights(2)
            sp.dma_start(bvb[:, :], bv.rearrange("(a d) -> a d", a=1).broadcast_to([P, D])).then_inc(bias_in, 16)
            sp.wait_ge(blank_made, 1)
            for at in (0, 32):
                sp.dma_start(b1rows[at:at + E, :], b1).then_inc(bias_in, 16)
            sp.dma_start(slots_v, blank[:, None, :].broadcast_to([P, TILES, ROW // 2])).then_inc(blank_sent, 16)
            sp.dma_start(wts_f[:, :, KIT_AT // 2 + B2F:KIT_AT // 2 + B2F + D],
                         b2.rearrange("(a e) d -> a e d", a=1).broadcast_to([P, E, D])).then_inc(b2_in, 16)

            def load_kit(j):
                e = nc.s_assert_within(
                    sp.value_load(expert[j:j + 1, 0:1]), 0, min(j, E - 1),
                    skip_runtime_bounds_check_because="every expert has a tile")
                if j < E:
                    sp.wait_ge(wlo_done, j + 1)
                if j >= NST:
                    sp.wait_ge(y_done, j - NST + 1)
                sp.dma_start(stage_i[:, j % NST, :],
                             wts_i[:, bass.ds(e, 1), KIT_AT // 2:EW // 2].rearrange("p a c -> p (a c)")).then_inc(staged[j % NST], 16)

            load_weights(RAW // 2)
            sp.wait_ge(expert_done, 1)
            sp.wait_ge(b2_in, 16)
            sp.wait_ge(blank_sent, 16)
            for n in range(RAW // 2, E // 2 - 1):
                for j in range(2 * n - RAW, min(2 * n - RAW + 2, NST - 1)):
                    load_kit(j)
                if n + 1 < E // 2 - 1:
                    load_weights(n + 1)
            sp.wait_ge(rows_sent, 16 * K * NT)
            for n, (a, z) in enumerate(zip(XG, XG[1:])):
                sp.dma_start(slots_i[:, a:z, :], slots_v[:, a:z, :]).then_inc(slots_in[n], 16)
                if n == 0:
                    load_weights(len(WL) - 3)
                    load_kit(NST - 1)
                    load_weights(len(WL) - 2)
            for j in range(NST, TILES):
                load_kit(j)
            for n in range(NYB):
                sp.wait_ge(y_sent[n], 16 * len(range(n, TILES, NYB)))
            for n in range(NYL):
                sp.dma_start(pairs[:, TYL * n:TYL * n + TYL, :, :],
                             pairs_v[:, TYL * n:TYL * n + TYL, :, :]).then_inc(pairs_in[n], 16)
            for n in range(NYL):
                if n in POOL_SUMS:
                    sp.wait_ge(res_pool, POOL_SUMS.index(n) + 1)
                else:
                    sp.wait_ge(res_done, SUMS.index(n) + 1)
                if n == NYL - 1:
                    sp.wait_ge(o_read, NT)
                sp.dma_start(out_v[:, TYL * n:TYL * n + TYL, :], xin[:, TYL * n:TYL * n + TYL, :]).then_inc(out_sent, 16)
            sp.wait_ge(out_sent, 16 * NYL)

        @block.gpsimd
        def _(pool):
            made = [0]

            def step(ins):
                made[0] += 1
                ins.then_inc(pool_step, 1)
                pool.wait_ge(pool_step, made[0])

            pool.memset(epsc[:, :], EPS)
            step(pool.memset(ident[:, :], 0.0))
            pool.affine_select(out=ident[:, :], in_=ident[:, :], compare_op=ALU.not_equal, fill=1.0,
                               base=0, pattern=[[-1, P]], channel_multiplier=1).then_inc(ident_made, 1)
            pool.memset(b1rows[:, :], 0.0)
            pool.memset(wscale[:, :], 0.0)
            step(pool.memset(blank[:, :].bitcast(F32), 0.0))
            pool.iota(blank[:, D:D + 1], pattern=[[0, 1]], base=1 << 20,
                      channel_multiplier=0).then_inc(blank_made, 1)
            pool.memset(later[:, :], 0.0)
            for e in range(E):
                pool.memset(rev[:, e, :], float(E - e))
            pool.memset(keep[:, :, 1:NT], 1.0)
            pool.memset(keep[:, :, 0:1], 0.0)
            pool.memset(ones16[:, :], 1.0)
            step(pool.memset(ones[:, :], 1.0))
            pool.affine_select(out=later[:, :], in_=later[:, :], compare_op=ALU.is_gt, fill=-1.0,
                               base=0, pattern=[[1, P]], channel_multiplier=-1)
            for k in range(K):
                pool.iota(rows_i[:, k, :, D:D + 1], pattern=[[K * P, NT], [0, 1]], base=k, channel_multiplier=K)
            pool.memset(causal[:, :], 0.0)
            step(pool.iota(scratch_i[:, :], pattern=[[0, 1]], base=0, channel_multiplier=1))
            pool.tensor_copy(tileno[:, :], scratch_i[:, :])
            pool.affine_select(out=causal[:, S - P:], in_=causal[:, S - P:], compare_op=ALU.is_ge, fill=-HUGE,
                               base=0, pattern=[[-1, P]], channel_multiplier=1)
            pool.tensor_copy(ident16[:, :], ident[:, :]).then_inc(consts, 1)
            for parts in b1parts:
                pool.memset(parts[:, :], 0.0)
            step(pool.tensor_copy(diag[:, :], ident[:, 0:E]))
            pool.tensor_tensor(diag[:, :], diag[:, :], ident[:, 32:32 + E], ALU.add).then_inc(consts, 1)
            sel = wts[:, :, KIT_AT + SEL:KIT_AT + SEL + P]
            step(pool.memset(sel, 0.0))

            def rows_lo(g):
                here = slice(G * g, G * g + G)
                pool.wait_ge(hi_rows, g + 1)
                pool.tensor_tensor(rows[:, 0, here, D:2 * D], xn[:, here, :], rows[:, 0, here, 0:D],
                                   ALU.subtract).then_inc(lo_rows, 1)

            for half in range(2):
                rows_lo(half)
                step(pool.affine_select(out=sel, in_=sel, compare_op=ALU.not_equal, fill=1.0,
                                        base=-32 * half, pattern=[[-1, E], [0, P]], channel_multiplier=1))
            for g in range(2, NG):
                rows_lo(g)
            def high(n):
                e = POOL_HIGH[n]
                pool.wait_ge(scale_done, e // WG + 1)
                pool.tensor_tensor(high_part(e), raw[:, e % RAW, :, :],
                                   wscale[:, e:e + 1, None].broadcast_to([P, 2, HID]), ALU.mult).then_inc(whi_pool, 1)

            pool.wait_ge(bias_in, 16 * 3)
            for g in range(NG):
                pool.wait_ge(xn_done, g + 1)
                here = slice(G * g, G * g + G)
                pool.tensor_tensor(xin[:, here, :], xin[:, here, :], bvb[:, None, :].broadcast_to([P, G, D]),
                                   ALU.add).then_inc(xbv_done, 1)
            for n in range(2):
                high(n)
            pool.wait_ge(blank_sent, 16)
            pool.wait_ge(lo_rows, NG)
            pool.wait_ge(slotrow_done, 1)
            for k in range(K):
                if k == 1:
                    pool.wait_ge(rows_done, 1)
                for t in range(NT):
                    pool.indirect_dma_start(slots_dram, bass.IndirectOffsetOnAxis(ap=slotrow[:, k, t:t + 1], axis=0),
                                            rows_i[:, k, t, :], None).then_inc(rows_sent, 16)
            high(2)
            high(3)
            for j in range(TILES):
                if j in POOL_HIGH_LATE:
                    high(POOL_HIGH_LATE[j])
                if j in XG:
                    pool.wait_ge(slots_in[XG.index(j)], 16)
                pool.wait_ge(y_gated, j + 1)
                pool.indirect_dma_start(pairs_dram, bass.IndirectOffsetOnAxis(ap=slots_i[:, j, D:D + 1], axis=0),
                                        ybuf[:, j % NYB, :], None, bounds_check=NT * P * K - 1,
                                        oob_is_err=False).then_inc(y_sent[j % NYB], 16)
            for n in POOL_SUMS:
                pool.wait_ge(o_read, TYL * n + TYL)
                pool.wait_ge(pairs_in[n], 16)
                here = slice(TYL * n, TYL * n + TYL)
                for k in range(K):
                    ins = pool.tensor_tensor(xin[:, here, :], xin[:, here, :], pairs[:, here, k, :], ALU.add)
                    if k + 1 < K:
                        step(ins)
                ins.then_inc(res_pool, 1)

        @block.scalar
        def _(act):
            act.wait_ge(ident_made, 1)

            def std_of(g):
                act.wait_ge(var_done, g + 1)
                nc.scalar.activation(std[:, G * g:G * g + G], mv[:, G * g:G * g + G, 1], ACT.Sqrt,
                                     bias=epsc[:, :]).then_inc(std_done, 1)

            def xT_copy(g):
                act.wait_ge(xT_done, g + 1)
                nc.scalar.copy(xT[:, G * P * g:G * P * (g + 1)], pT[g % 2][:, :]).then_inc(xT_copied, 1)

            def rows_hi(g):
                act.wait_ge(xn_done, g + 1)
                nc.scalar.copy(rows[:, 0, G * g:G * g + G, 0:D], xn[:, G * g:G * g + G, :]).then_inc(hi_rows, 1)

            for g in range(NG):
                std_of(g)
                if g == 0:
                    act.wait_ge(wT_done, 1)
                    nc.scalar.copy(wqkvT[:, :, :],
                                   pO[1][:, 0:3 * D].rearrange("p (n d) -> p n d", n=3)).then_inc(wT_copied, 1)
                if g:
                    xT_copy(g - 1)
                    rows_hi(g - 1)
            xT_copy(NG - 1)
            rows_hi(NG - 1)

            def squares(e):
                act.wait_ge(w_in[sum(z <= e for z in WL[1:])], 32)
                nc.scalar.activation(low_part(e), raw[:, e % RAW, :, :], ACT.Square, scale=16.0,
                                     accum_out=sumsq[:, e:e + 1]).then_inc(sq_done, 1)

            squares(0)
            squares(1)
            act.wait_ge(proj_in, 16 * 5)
            for g in range(NG):
                for n, to in enumerate((qT, kT)):
                    act.wait_ge(proj_done, 3 * g + n + 1)
                    nc.scalar.activation(to[:, G * P * g:G * P * (g + 1)], pA(3 * g + n), ACT.Identity,
                                         bias=bqk[:, n:n + 1]).then_inc(proj_copied, 1)
                act.wait_ge(proj_done, 3 * g + 3)
                nc.scalar.copy(v[:, G * g:G * g + G, :],
                               pA(3 * g + 2).rearrange("p (t d) -> p t d", t=G)).then_inc(proj_copied, 1)
                squares(2 + g)
                if g == 1:
                    act.wait_ge(gap_done, 1)
                    nc.scalar.activation(ex[:, :, :], ex[:, :, :], ACT.Exp)
                    nc.scalar.activation(gap[:, :], gap[:, :], ACT.Exp).then_inc(ex_done, 1)

            def high(e):
                act.wait_ge(scale_done, e // WG + 1)
                nc.scalar.activation(high_part(e), raw[:, e % RAW, :, :], ACT.Copy,
                                     scale=wscale[:, e:e + 1]).then_inc(whi_act, 1)

            def softmax(t):
                n = (t % TB + 1) * P
                act.wait_ge(max_done, t + 1)
                if t == 0:
                    act.wait_ge(lo_rows, NG)
                if t >= 2:
                    act.wait_ge(pt_done, groups_until(t - 1))
                nc.scalar.activation(probs[:, t % 2, 0:n], pS[t % 2][:, 0:n], ACT.Exp, bias=negm[:, t:t + 1],
                                     scale=-1.0, accum_out=rsum[:, t:t + 1]).then_inc(exp_done, 1)

            def probsT_copy(t):
                u = groups_until(t)
                n = min(t % TB + 1, G) * P
                act.wait_ge(pt_done, u + 1)
                if t >= 2:
                    act.wait_ge(o_done, t - 1)
                nc.scalar.copy(probsT[t % 2][:, 0, 0:n], pT[0][:, 0:n]).then_inc(pt_act, 1)

            def b1_high(n):
                act.wait_ge(b1s_done, n + 1)
                nc.scalar.activation(b1parts[n][0:32 + E, :], b1rows[0:32 + E, :], ACT.Copy,
                                     scale=b1s[0:32 + E, :]).then_inc(b1hi_done, 1)

            def attention(a, z):
                softmax(a)
                softmax(a + 1)
                probsT_copy(a)
                for t in range(a, z):
                    if t + 1 < z:
                        probsT_copy(t + 1)
                    if t + 2 < z:
                        softmax(t + 2)
                    if t == B1_AT + 1:
                        b1_high(0)
                    for e in SQUARES.get(t, ()):
                        squares(e)
                    for e in HIGH.get(t, ()):
                        high(e)

            attention(0, NT - LATE)
            def xs_copy(j):
                act.wait_ge(xs_done, j + 1)
                if j >= 3:
                    act.wait_ge(l1_done, j - 2)
                nc.scalar.copy(xslot[:, j % 3, :], pT[j % 2][:, :].bitcast(F16)[:, 0:2 * D]).then_inc(xs_copied, 1)

            def gated(r):
                act.wait_ge(y_done, r + 1)
                if r in XG:
                    act.wait_ge(slots_in[XG.index(r)], 16)
                nc.scalar.activation(ybuf[:, r % NYB, :], ybuf[:, r % NYB, :], ACT.Copy,
                                     scale=slots_f[:, r, D + 1:D + 2]).then_inc(y_gated, 1)

            xs_copy(0)
            xs_copy(1)
            for e in SQUARES_LATE[-1]:
                squares(e)
            for j in range(TILES):
                act.wait_ge(l1_done, j + 1)
                if j >= NHB:
                    act.wait_ge(l2_done, j - NHB + 1)
                nc.scalar.activation(hid[:, j % NHB, 0, :], pA(j), ACT.Relu).then_inc(hi_done, 1)
                if j + 2 < TILES:
                    xs_copy(j + 2)
                for e in SQUARES_LATE.get(j, ()):
                    squares(e)
                for e in HIGH_LATE.get(j, ()):
                    high(e)
                if j == B1_HIGH_LATE:
                    b1_high(1)
                if j >= 3:
                    gated(j - 3)
            for r in range(TILES - 3, TILES):
                gated(r)
            attention(NT - LATE, NT)

        @block.vector
        def _(dve):
            made = [0]

            def step(ins):
                made[0] += 1
                ins.then_inc(dve_step, 1)
                dve.wait_ge(dve_step, made[0])

            def moments(g):
                dve.wait_ge(x_in[g], 16)
                for t in range(G * g, G * g + G):
                    ins = dve.bn_stats(stats[:, t, :], xin[:, t, :])
                step(ins)
                for t in range(G * g, G * g + G):
                    ins = dve.bn_aggr(mv[:, t, :], stats[:, t, :])
                ins.then_inc(var_done, 1)

            def normalise(g):
                dve.wait_ge(std_done, g + 1)
                step(dve.reciprocal(rstd[:, G * g:G * g + G], std[:, G * g:G * g + G]))
                for t in range(G * g, G * g + G):
                    ins = dve.tensor_scalar(xn[:, t, :], xin[:, t, :], mv[:, t, 0:1], rstd[:, t:t + 1],
                                            ALU.subtract, ALU.mult)
                ins.then_inc(xn_done, 1)

            def b1_norms():
                dve.wait_ge(b1cols_in, 16)
                step(dve.tensor_tensor(b1sq[:, :, :], b1cols[:, :, :], b1cols[:, :, :], ALU.mult))
                step(dve.tensor_reduce(b1sum[:, :], b1sq[:, :, :], AX.X, ALU.add))
                dve.tensor_scalar(b1sum[:, :], b1sum[:, :], 2.0 ** -120, None, ALU.max).then_inc(b1sum_done, 1)

            def scales(g, z):
                s = slice(WG * g, WG * z)
                dve.wait_ge(sums_done, z)
                step(dve.tensor_scalar(expo[:, s], sums_bank(g)[:, s].bitcast(I32), 1, None, ALU.logical_shift_right))
                step(dve.tensor_scalar(expo2[:, s], expo[:, s], float(127 << 22), None, ALU.add))
                step(dve.tensor_scalar(pw[:, s], expo2[:, s], 0xFF << 23, None, ALU.bitwise_and))
                dve.tensor_scalar(wscale[:, s].bitcast(I32), pw[:, s], -1.0, float((254 + 13) << 23), ALU.mult,
                                  ALU.add).then_inc(scale_done, z - g)
                dve.scalar_tensor_tensor(out=wts_f[:, s, KIT_AT // 2 + CF], in0=pw[:, s].bitcast(F32),
                                         scalar=2.0 ** -26, in1=pw[:, s].bitcast(F32),
                                         op0=ALU.mult, op1=ALU.mult)

            moments(0)
            for g in range(NG):
                if g + 1 < NG:
                    moments(g + 1)
                normalise(g)

            b1_norms()

            dve.wait_ge(router_in, 32)
            dve.wait_ge(consts, 1)
            dve.wait_ge(logits_done, NG)

            def over_tiles(a):
                return a[:, :, None].broadcast_to([P, E, NT])

            def over_experts(a):
                return a[:, None, :].broadcast_to([P, E, NT])

            def flat(a):
                return a.rearrange("p e t -> p (e t)")

            def by_token(a):
                return a.rearrange("p e t -> p t e")

            step(dve.tensor_tensor(lg[:, :, :], pO[0][:, 0:NT * E].rearrange("p (t e) -> p e t", e=E),
                                   over_tiles(brb[:, :]), ALU.add))
            step(dve.tensor_reduce(best[:, 0, :], by_token(lg[:, :, :]), AX.X, ALU.max))
            for k, logits in enumerate((lg, lg2)):
                step(dve.tensor_tensor(hit[:, :, :], logits[:, :, :], over_experts(best[:, k, :]), ALU.is_equal))
                step(dve.tensor_tensor(hit[:, :, :], hit[:, :, :], rev[:, :, :], ALU.mult))
                step(dve.tensor_reduce(pick[:, :], by_token(hit[:, :, :]), AX.X, ALU.max))
                step(dve.tensor_tensor(oh[:, k, :, :], rev[:, :, :], over_experts(pick[:, :]), ALU.is_equal))
                if k == 0:
                    step(dve.scalar_tensor_tensor(out=lg2[:, :, :], in0=oh[:, 0, :, :], scalar=-HUGE,
                                                  in1=lg[:, :, :], op0=ALU.mult, op1=ALU.add))
                    step(dve.tensor_reduce(best[:, 1, :], by_token(lg2[:, :, :]), AX.X, ALU.max))
            step(dve.tensor_tensor(chosen[:, :, :], oh[:, 0, :, :], oh[:, 1, :, :], ALU.add))
            dve.tensor_tensor_scan(flat(sofar[:, :, :]), flat(keep[:, :, :]), flat(chosen[:, :, :]), 0.0, ALU.mult,
                                   ALU.add).then_inc(chosen_done, 1)
            dve.tensor_tensor(ex[:, :, :], lg[:, :, :], over_experts(best[:, 0, :]), ALU.subtract)
            dve.tensor_tensor(gap[:, :], best[:, 1, :], best[:, 0, :], ALU.subtract).then_inc(gap_done, 1)
            scales(0, 1)

            dve.wait_ge(ranks_done, 1)
            rank = pO[0][:, 0:E * NT].rearrange("p (e t) -> p e t", e=E)
            total = pO[0][:, E * NT:E * NT + E]
            step(dve.tensor_scalar(cnt[:, :], total, 1.0, float(P - 1), ALU.max, ALU.add))
            step(dve.tensor_scalar(ntile[:, :], cnt[:, :], P.bit_length() - 1, None, ALU.logical_shift_right))
            step(dve.tensor_copy(ntilef[:, :], ntile[:, :]))
            step(dve.tensor_tensor_scan(cum[:, :], ones[:, 0:E], ntilef[:, :], 0.0, ALU.mult, ALU.add))
            step(dve.tensor_tensor(start[:, :], cum[:, :], ntilef[:, :], ALU.subtract))
            step(dve.scalar_tensor_tensor(out=pos[:, :, :], in0=over_tiles(start[:, :]), scalar=float(P),
                                          in1=rank, op0=ALU.mult, op1=ALU.add))
            step(dve.tensor_tensor(oh[:, :, :, :], oh[:, :, :, :],
                                   pos[:, None, :, :].broadcast_to([P, K, E, NT]), ALU.mult))
            step(dve.tensor_reduce(posk[:, :, :], oh[:, :, :, :].rearrange("p k e t -> p k t e"), AX.X, ALU.add))
            dve.wait_ge(ex_done, 1)
            step(dve.tensor_reduce(exsum[:, :], by_token(ex[:, :, :]), AX.X, ALU.add))
            step(dve.reciprocal(rows_f[:, 0, :, D + 1], exsum[:, :]))
            dve.tensor_tensor(rows_f[:, 1, :, D + 1], rows_f[:, 0, :, D + 1], gap[:, :], ALU.mult)
            step(dve.tensor_copy(posi[:, :, :], posk[:, :, :]))
            dve.tensor_scalar(posr[:, :, :], posi[:, :, :], P.bit_length() - 1, None, ALU.logical_shift_right)
            step(dve.tensor_scalar(posi[:, :, :], posi[:, :, :], P - 1, None, ALU.bitwise_and))
            dve.scalar_tensor_tensor(out=slotrow[:, :, :], in0=posi[:, :, :], scalar=float(TILES),
                                     in1=posr[:, :, :], op0=ALU.mult, op1=ALU.add).then_inc(slotrow_done, 1)

            def low(e):
                if e in POOL_HIGH:
                    dve.wait_ge(whi_pool, POOL_HIGH.index(e) + 1)
                else:
                    dve.wait_ge(whi_act, sum(a not in POOL_HIGH for a in range(e + 1)))
                dve.wait_ge(scale_done, e // WG + 1)
                dve.scalar_tensor_tensor(out=low_part(e), in0=raw[:, e % RAW, :, :], scalar=wscale[:, e:e + 1],
                                         in1=high_part(e), op0=ALU.mult, op1=ALU.subtract).then_inc(wlo_done, 1)

            def row_max(t):
                n = (t % TB + 1) * P
                dve.wait_ge(s_done, t + 1)
                dve.tensor_tensor_reduce(out=pS[t % 2][:, 0:n], in0=pS[t % 2][:, 0:n], in1=causal[:, S - n:],
                                         scale=-SCALE, scalar=HUGE, op0=ALU.add, op1=ALU.min,
                                         accum_out=negm[:, t:t + 1]).then_inc(max_done, 1)

            def probsT_copy(t):
                if t % TB + 1 > G:
                    n = (t % TB + 1 - G) * P
                    dve.wait_ge(pt_done, groups_until(t) + 2)
                    if t >= 2:
                        dve.wait_ge(o_done, t - 1)
                    dve.tensor_copy(probsT[t % 2][:, 1, 0:n], pT[1][:, 0:n]).then_inc(pt_dve, 1)

            def inverse_sum(t):
                dve.wait_ge(exp_done, t + 1)
                dve.reciprocal(rinv[:, t:t + 1], rsum[:, t:t + 1]).then_inc(rinv_done, 1)

            def attended(t):
                dve.wait_ge(rinv_done, t + 1)
                dve.wait_ge(o_done, t + 1)
                dve.wait_ge(xbv_done, t // G + 1)
                dve.scalar_tensor_tensor(out=xin[:, t, :], in0=pO[t % 2][:, 0:D], scalar=rinv[:, t:t + 1],
                                         in1=xin[:, t, :], op0=ALU.mult, op1=ALU.add).then_inc(o_read, 1)

            def b1_factors(groups):
                dve.wait_ge(consts, 2)
                dve.wait_ge(scale_done, groups)
                step(dve.tensor_tensor(b1tmp[0:32 + E, :], wscale[0:32 + E, :], diag[0:32 + E, :], ALU.mult))
                dve.tensor_reduce(b1s[0:32 + E, :], b1tmp[0:32 + E, :], AX.X, ALU.add).then_inc(b1s_done, 1)

            def experts_of_tiles():
                step(dve.tensor_scalar(past[:, :], cum[:, :], tileno[:, :], None, ALU.is_le))
                step(dve.tensor_reduce(expertf[:, :], past[:, :], AX.X, ALU.add))
                dve.tensor_scalar(expert[:, :], expertf[:, :], float(E - 1), None, ALU.min).then_inc(expert_done, 1)

            def b1_low(n):
                dve.wait_ge(b1hi_done, n + 1)
                dve.scalar_tensor_tensor(out=b1parts[n][32:32 + E, :], in0=b1rows[32:32 + E, :],
                                         scalar=b1s[32:32 + E, :], in1=b1parts[n][32:32 + E, :], op0=ALU.mult,
                                         op1=ALU.subtract).then_inc(b1_done, 1)

            def attention(a, z):
                row_max(a)
                row_max(a + 1)
                probsT_copy(a)
                for t in range(a, z):
                    if t + 2 < z:
                        row_max(t + 2)
                    if t == 0:
                        scales(1, 3)
                        experts_of_tiles()
                        dve.wait_ge(lo_rows, NG)
                        dve.tensor_copy(rows[:, 1, :, 0:2 * D], rows[:, 0, :, 0:2 * D]).then_inc(rows_done, 1)
                    if t == B1_AT + 2:
                        b1_low(0)
                    inverse_sum(t)
                    if t == NT - 2:
                        combine(SUMS[0])
                        combine(SUMS[1])
                    if t + 1 < z:
                        probsT_copy(t + 1)
                    if t > a and t < NT - 1:
                        attended(t - 1)
                    for e in LOW.get(t, ()):
                        low(e)
                    if t > 0:
                        for g in SCALES.get(t + 1, ()):
                            scales(g, g + 1)
                    if t == B1_AT:
                        b1_factors(GROUPS_LATE[0])
                if z < NT:
                    attended(z - 1)

            attention(0, NT - LATE)
            low(10)

            def y_of(j):
                dve.wait_ge(l2_done, j + 1)
                dve.wait_ge(staged[j % NST], 16 * (j // NST + 1))
                if j >= NYB:
                    dve.wait_ge(y_sent[j % NYB], 16 * (j // NYB))
                dve.scalar_tensor_tensor(out=ybuf[:, j % NYB, :], in0=pO[j % 2][:, 0:D],
                                         scalar=stage_f[:, j % NST, CF:CF + 1],
                                         in1=stage_f[:, j % NST, B2F:B2F + D],
                                         op0=ALU.mult, op1=ALU.add).then_inc(y_done, 1)

            for j in range(TILES):
                if j == SCALES_LATE:
                    scales(GROUPS_LATE[0], GROUPS_LATE[-1] + 1)
                    b1_factors(GROUPS_LATE[-1] + 1)
                dve.wait_ge(hi_done, j + 1)
                dve.scalar_tensor_tensor(out=hid[:, j % NHB, 1, :], in0=pA(j), scalar=0.0,
                                         in1=hid[:, j % NHB, 0, :], op0=ALU.max,
                                         op1=ALU.subtract).then_inc(lo_done, 1)
                if j >= 2:
                    y_of(j - 2)
                for e in LOW_LATE.get(j, ()):
                    low(e)
                if j == B1_LOW_LATE:
                    b1_low(1)
            y_of(TILES - 2)
            y_of(TILES - 1)

            def combine(n):
                dve.wait_ge(pairs_in[n], 16)
                here = slice(TYL * n, TYL * n + TYL)
                for k in range(K):
                    ins = dve.tensor_tensor(xin[:, here, :], xin[:, here, :], pairs[:, here, k, :], ALU.add)
                    if k + 1 < K:
                        step(ins)
                ins.then_inc(res_done, 1)

            attention(NT - LATE, NT)
            for n in SUMS[2:-1]:
                combine(n)
            attended(NT - 2)
            dve.wait_ge(o_read, NT - 1)
            combine(SUMS[-1])
            dve.wait_ge(res_done, len(SUMS))
            attended(NT - 1)

        @block.tensor
        def _(pe):
            pe.wait_ge(ident_made, 1)

            def weight_sums(g, z):
                pe.wait_ge(sq_done, WG * z)
                if g:
                    pe.wait_ge(scale_done, g)
                s = slice(WG * g, WG * z)
                pe.matmul(sums_bank(g)[:, s], ones[:, :], sumsq[:, s], start=True, stop=False)
                pe.matmul(sums_bank(g)[:, s], ones[:, :], b1sum[:, s], start=False, stop=True).then_inc(sums_done, z - g)

            def x_transposes(g):
                pe.wait_ge(xn_done, g + 1)
                if g >= 2:
                    pe.wait_ge(xT_copied, g - 1)
                for i in range(G):
                    ins = pe.transpose(pT[g % 2][:, i * P:(i + 1) * P], xn[:, G * g + i, :], ident[:, :])
                ins.then_inc(xT_done, 1)

            def router(g):
                pe.wait_ge(xT_copied, g + 1)
                for t in range(G * g, G * g + G):
                    ins = pe.matmul(pO[0][:, t * E:(t + 1) * E], xT[:, t * P:(t + 1) * P], wr[:, :],
                                    start=True, stop=True)
                ins.then_inc(logits_done, 1)

            def keep_busy(n):
                for _ in range(n):
                    pe.matmul(pA(0)[:, 0:P], ident[:, :], ident[:, :], start=True, stop=True)

            keep_busy(WARM_UP)
            pe.wait_ge(proj_in, 16 * 5)
            for n in range(3):
                ins = pe.transpose(pO[1][:, n * D:(n + 1) * D], wqkv[:, n, :], ident[:, :])
            ins.then_inc(wT_done, 1)
            for g in range(NG):
                x_transposes(g)
                if g == 0:
                    keep_busy(8)
                if g == 1:
                    pe.wait_ge(router_in, 32)
                if g:
                    router(g - 1)
                if g == 1:
                    keep_busy(4)
            router(NG - 1)

            pe.wait_ge(consts, 1)
            pe.wait_ge(wT_copied, 1)
            for g in range(NG):
                cols = slice(G * P * g, G * P * (g + 1))
                for n in range(3):
                    if 3 * g + n >= 4:
                        pe.wait_ge(proj_copied, 3 * g + n - 3)
                    if n < 2:
                        ins = pe.matmul(pA(3 * g + n), wqkvT[:, n, :], xT[:, cols], start=True, stop=True)
                    else:
                        for i in range(G):
                            t = G * g + i
                            ins = pe.matmul(pA(3 * g + 2)[:, i * D:(i + 1) * D], xT[:, t * P:(t + 1) * P],
                                            wqkvT[:, 2, :], start=True, stop=True)
                    ins.then_inc(proj_done, 1)
                if g == 1:
                    pe.wait_ge(chosen_done, 1)
                    flat = "p e t -> p (e t)"
                    pe.matmul(pO[0][:, 0:E * NT], later[:, :], chosen[:, :, :].rearrange(flat), start=True,
                              stop=False)
                    pe.matmul(pO[0][:, 0:E * NT], ones16[:, :], sofar[:, :, :].rearrange(flat), start=False,
                              stop=True)
                    pe.matmul(pO[0][:, E * NT:E * NT + E], ones16[:, :], sofar[:, :, NT - 1], start=True,
                              stop=True).then_inc(ranks_done, 1)
                    pe.wait_ge(b1sum_done, 1)
                    weight_sums(0, 1)

            def scores(t):
                n = (t % TB + 1) * P
                if t >= 2:
                    pe.wait_ge(exp_done, t - 1)
                if t == NT - LATE:
                    pe.wait_ge(lo_done, TILES)
                if t == 0:
                    pe.wait_ge(proj_copied, 3 * NG)
                at = t // TB * S
                for a in range(0, n, 512):
                    z = min(a + 512, n)
                    ins = pe.matmul(pS[t % 2][:, a:z], qT[:, t * P:(t + 1) * P], kT[:, at + a:at + z],
                                    start=True, stop=True)
                ins.then_inc(s_done, 1)

            def probs_transposes(t):
                pe.wait_ge(exp_done, t + 1)
                if t >= 1:
                    pe.wait_ge(pt_act, t)
                    second = sum(u % TB + 1 > G for u in range(t))
                    if second:
                        pe.wait_ge(pt_dve, second)
                for a in range(0, t % TB + 1, G):
                    for j in range(a, min(a + G, t % TB + 1)):
                        ins = pe.transpose(pT[a // G][:, (j - a) * P:(j - a + 1) * P],
                                           probs[:, t % 2, j * P:(j + 1) * P], ident[:, :])
                    ins.then_inc(pt_done, 1)

            def attend(t):
                i = t % TB
                pe.wait_ge(pt_act, t + 1)
                if i + 1 > G:
                    pe.wait_ge(pt_dve, sum(u % TB + 1 > G for u in range(t + 1)))
                if t >= 2:
                    pe.wait_ge(o_read, t - 1)
                if t >= NT - LATE:
                    pe.wait_ge(y_done, TILES)
                if t == 0:
                    pe.wait_ge(slotrow_done, 1)
                for g in SCALES.get(t, ()):
                    pe.wait_ge(scale_done, g + 1)
                for j in range(i + 1):
                    ins = pe.matmul(pO[t % 2][:, 0:D], probsT[t % 2][:, j // G, j % G * P:(j % G + 1) * P],
                                    v[:, t // TB * TB + j, :], start=(j == 0), stop=(j == i))
                ins.then_inc(o_done, 1)

            def attend_after(a, z):
                probs_transposes(a)
                if a + 2 < z:
                    scores(a + 2)
                for t in range(a, z):
                    if t + 1 < z:
                        probs_transposes(t + 1)
                    if t + 3 < z:
                        scores(t + 3)
                    if t > 0:
                        for g in SCALES.get(t + 1, ()):
                            pe.wait_ge(o_read, t)
                            weight_sums(g, g + 1)
                    attend(t)

            scores(0)
            scores(1)
            weight_sums(1, 3)
            attend_after(0, NT - LATE)

            def slot_transposes(j):
                if j in XG:
                    pe.wait_ge(slots_in[XG.index(j)], 16)
                if j < 2:
                    pe.wait_ge(pt_act, NT - LATE)
                if j == SCALES_LATE + 2:
                    pe.wait_ge(scale_done, GROUPS_LATE[-1] + 1)
                to = pT[j % 2][:, :].bitcast(F16)
                pe.transpose(to[:, 0:D], slots[:, j, 0:D], ident16[:, :])
                pe.transpose(to[:, D:2 * D], slots[:, j, D:2 * D], ident16[:, :]).then_inc(xs_done, 1)

            def expert_of(j):
                return nc.s_assert_within(
                    pe.value_load(expert[j:j + 1, 0:1]), 0, min(j, E - 1),
                    skip_runtime_bounds_check_because="every expert has a tile")

            def result(r, c):
                s = stage[:, r % NST, :]
                y = pO[r % 2][:, 0:D]
                h_hi, h_lo = hid[:, r % NHB, 0, c * P:(c + 1) * P], hid[:, r % NHB, 1, c * P:(c + 1) * P]
                w_hi, w_lo = s[:, W2_HI + c * P:W2_HI + (c + 1) * P], s[:, W2_LO + c * P:W2_LO + (c + 1) * P]
                pe.matmul(y, h_hi, w_hi, start=(c == 0), stop=False)
                pe.matmul(y, h_hi, w_lo, start=False, stop=False)
                return pe.matmul(y, h_lo, w_hi, start=False, stop=(c == NCH - 1))

            def result_waits(r):
                pe.wait_ge(lo_done, r + 1)
                if r >= 2:
                    pe.wait_ge(y_done, r - 1)
                else:
                    pe.wait_ge(o_read, NT - LATE)

            def hidden(j, e, r):
                pe.wait_ge(xs_copied, j + 1)
                pe.wait_ge(staged[j % NST], 16 * (j // NST + 1))
                if j == SCALES_LATE:
                    weight_sums(GROUPS_LATE[0], GROUPS_LATE[-1] + 1)
                if j == B1_SECOND:
                    pe.wait_ge(b1_done, 2)
                bank = pA(j)
                x_hi, x_lo = xslot[:, j % 3, 0:D], xslot[:, j % 3, D:2 * D]
                for c in range(NCH):
                    pe.matmul(bank[:, c * P:(c + 1) * P], b1parts[j >= B1_SECOND][:, c:HID:NCH],
                              stage[:, j % NST, SEL:SEL + P], start=(c == 0), stop=False, skip_group_check=True)
                after = None
                for c in range(NCH):
                    to = bank[:, c * P:(c + 1) * P]
                    w_hi = wts[:, bass.ds(e, 1), W1_HI + c:W1_HI + HID:NCH].rearrange("p a h -> p (a h)")
                    pe.matmul(to, w_hi, x_hi, start=False, stop=False, skip_group_check=True)
                    pe.matmul(to, w_hi, x_lo, start=False, stop=False, skip_group_check=True)
                    w_lo = wts[:, bass.ds(e, 1), W1_LO + c:W1_LO + HID:NCH].rearrange("p a h -> p (a h)")
                    ins = pe.matmul(to, w_lo, x_hi, start=False, stop=(c == NCH - 1), skip_group_check=True)
                    if c == 1 and j + 1 < TILES:
                        after = expert_of(j + 1)
                    if r is not None:
                        if c == 1:
                            result_waits(r)
                            result(r, 0)
                            result(r, 1)
                        elif c > 1:
                            last = result(r, c)
                ins.then_inc(l1_done, 1)
                if r is not None:
                    last.then_inc(l2_done, 1)
                return after

            pe.wait_ge(expert_done, 1)
            e = expert_of(0)
            slot_transposes(0)
            slot_transposes(1)
            pe.wait_ge(b1_done, 1)
            for j in range(TILES):
                e = hidden(j, e, j - 2 if j >= 2 else None)
                if j + 2 < TILES:
                    slot_transposes(j + 2)
            for r in (TILES - 2, TILES - 1):
                result_waits(r)
                for c in range(NCH):
                    last = result(r, c)
                last.then_inc(l2_done, 1)
            scores(NT - LATE)
            scores(NT - LATE + 1)
            attend_after(NT - LATE, NT)


_INS = ["L0_attn_x", "L0_attn_Wk", "L0_attn_bk", "L0_attn_Wq", "L0_attn_bq", "L0_attn_Wv", "L0_attn_bv",
        "L0_ffn_Wr", "L0_ffn_br", "L0_ffn_W1", "L0_ffn_b1", "L0_ffn_W2", "L0_ffn_b2"]


def kernel(**inputs):
    import numpy as np
    import concourse.bacc as bacc
    from concourse import mybir as mb
    from concourse.bass_utils import run_bass_kernel_spmd

    nc = bacc.Bacc("TRN2", target_bir_lowering=False, num_devices=1)
    arrays, args = {}, []
    for name in _INS:
        a = np.ascontiguousarray(inputs[name])
        arrays[f"in_{name}"] = a
        args.append(nc.dram_tensor(f"in_{name}", a.shape, mb.dt.from_np(a.dtype), kind="ExternalInput").ap())
    out = nc.dram_tensor("out_0", inputs["L0_attn_x"].shape, F32, kind="ExternalOutput").ap()
    attention_and_top2_experts(nc, *args, out)
    r = run_bass_kernel_spmd(nc, [arrays], core_ids=[0])
    return r.results[0]["out_0"]
```
